# Optimizing a Trainium2 kernel written in Bass

```python
import numpy as np
import jax
import jax.numpy as jnp

def _softmax(x, axis=-1):
    return jax.nn.softmax(x, axis=axis)

def _gelu(x):
    return jax.nn.gelu(x, approximate=True)

def _silu(x):
    return jax.nn.silu(x)

def _sigmoid(x):
    return jax.nn.sigmoid(x)

def _layernorm(x, axis=-1, eps=1e-05):
    m = jnp.mean(x, axis=axis, keepdims=True)
    v = jnp.var(x, axis=axis, keepdims=True)
    return (x - m) / jnp.sqrt(v + eps)

def _scatter_add(tgt, idx, src, axis=0):
    return tgt.at[idx].add(src)

def _segment_sum(src, seg, n):
    return jax.ops.segment_sum(src, seg, n)
kernel_name = 'mk_audio_tower_d2_tok_audfeat512_r4_609c74'

def setup_inputs(seed: int=0):
    np.random.seed(seed)
    _w = jnp.asarray

    def _rec_inputs():
        import jax
        import jax.numpy as jnp
        _rk = jax.random.key(seed)
        x = 7.22013e-05 + 1.00017 * jax.random.normal(jax.random.fold_in(_rk, 1), (8, 64, 750), jnp.float32)
        return x
    x = _rec_inputs()

    def _L0_tok_setup():
        import jax, jax.numpy as jnp
        import numpy as np
        B, C_IN, DIM, L = (8, 64, 128, 1024)

        def _layer_norm(y, gamma, beta, eps=1e-05):
            mu = jnp.mean(y, axis=-1, keepdims=True)
            var = jnp.mean(jnp.square(y - mu), axis=-1, keepdims=True)
            return (y - mu) * jax.lax.rsqrt(var + eps) * gamma + beta
        key = jax.random.key(seed)
        ks = jax.random.split(key, 4)
        x = jax.random.normal(ks[0], (B, C_IN, L), dtype=jnp.float32)
        W_proj = jax.random.normal(ks[1], (DIM, C_IN), dtype=jnp.float32) * (1.0 / np.sqrt(C_IN))
        b_proj = jnp.zeros((DIM,), dtype=jnp.float32)
        W_dw = jax.random.normal(ks[2], (DIM, 3), dtype=jnp.float32) * (1.0 / np.sqrt(3.0))
        b_dw = jnp.zeros((DIM,), dtype=jnp.float32)
        W_pw = jax.random.normal(ks[3], (DIM, DIM), dtype=jnp.float32) * (1.0 / np.sqrt(DIM))
        b_pw = jnp.zeros((DIM,), dtype=jnp.float32)
        gamma = jnp.ones((DIM,), dtype=jnp.float32)
        beta = jnp.zeros((DIM,), dtype=jnp.float32)
        return {'x': x, 'W_proj': W_proj, 'b_proj': b_proj, 'W_dw': W_dw, 'b_dw': b_dw, 'W_pw': W_pw, 'b_pw': b_pw, 'gamma': gamma, 'beta': beta}
    _L0_tok_all = _L0_tok_setup()
    _L0_tok_in = {k: v for k, v in _L0_tok_all.items() if k in ('W_proj', 'b_proj', 'W_dw', 'b_dw', 'W_pw', 'b_pw', 'gamma', 'beta')}
    del _L0_tok_all

    def _L0_attn_setup():
        import jax, jax.numpy as jnp
        import numpy as np
        D_MODEL = 128
        D_STATE = 16
        D_CONV = 4
        D_INNER = 256
        DT_RANK = 32
        B = 2
        L = 512

        def _mamba(x, W_in, conv_w, conv_b, W_xproj, W_dt, b_dt, A_log, D_skip, W_out):
            Bb, Ll, _ = x.shape
            xz = jnp.einsum('bld,ed->ble', x, W_in)
            xc, z = jnp.split(xz, 2, axis=-1)
            xp = jnp.pad(xc, ((0, 0), (D_CONV - 1, 0), (0, 0)))
            xc = conv_b + sum((xp[:, k:k + Ll, :] * conv_w[:, k] for k in range(D_CONV)))
            xc = jax.nn.silu(xc)
            proj = jnp.einsum('bld,ed->ble', xc, W_xproj)
            dt, Bm, Cm = jnp.split(proj, [DT_RANK, DT_RANK + D_STATE], axis=-1)
            dt = jax.nn.softplus(jnp.einsum('blr,dr->bld', dt, W_dt) + b_dt)
            A = -jnp.exp(A_log)

            def step(h, inp):
                dt_t, B_t, C_t, u_t = inp
                dA = jnp.exp(dt_t[..., None] * A)
                h = dA * h + dt_t[..., None] * B_t[:, None, :] * u_t[..., None]
                y = jnp.einsum('bdn,bn->bd', h, C_t)
                return (h, y)
            h0 = jnp.zeros((Bb, D_INNER, D_STATE), x.dtype)
            _, ys = jax.lax.scan(step, h0, (dt.swapaxes(0, 1), Bm.swapaxes(0, 1), Cm.swapaxes(0, 1), xc.swapaxes(0, 1)))
            y = ys.swapaxes(0, 1) + xc * D_skip
            y = y * jax.nn.silu(z)
            return jnp.einsum('ble,de->bld', y, W_out)

        def _block(x, fw, bw, ln_g, ln_b):
            f = _mamba(x, *fw)
            b = jnp.flip(_mamba(jnp.flip(x, 1), *bw), 1)
            out = (f + b) * 0.5
            mu = out.mean(-1, keepdims=True)
            var = ((out - mu) ** 2).mean(-1, keepdims=True)
            out = (out - mu) * jax.lax.rsqrt(var + 1e-05) * ln_g + ln_b
            return jax.nn.silu(out) + x

        def _params(key, pfx):
            ks = jax.random.split(key, 5)

            def n(k, shape, fan):
                return jax.random.normal(k, shape, jnp.float32) * fan ** (-0.5)
            return {pfx + 'W_in': n(ks[0], (2 * D_INNER, D_MODEL), D_MODEL), pfx + 'conv_w': n(ks[1], (D_INNER, D_CONV), D_CONV), pfx + 'conv_b': jnp.zeros((D_INNER,), jnp.float32), pfx + 'W_xproj': n(ks[2], (DT_RANK + 2 * D_STATE, D_INNER), D_INNER), pfx + 'W_dt': n(ks[3], (D_INNER, DT_RANK), DT_RANK), pfx + 'b_dt': jnp.full((D_INNER,), -4.0, jnp.float32), pfx + 'A_log': jnp.log(jnp.tile(jnp.arange(1, D_STATE + 1, dtype=jnp.float32), (D_INNER, 1))), pfx + 'D_skip': jnp.ones((D_INNER,), jnp.float32), pfx + 'W_out': n(ks[4], (D_MODEL, D_INNER), D_INNER)}
        key = jax.random.key(seed)
        k1, k2, k3 = jax.random.split(key, 3)
        inp = {'x': jax.random.normal(k1, (B, L, D_MODEL), jnp.float32)}
        inp.update(_params(k2, 'fw_'))
        inp.update(_params(k3, 'bw_'))
        inp['ln_g'] = jnp.ones((D_MODEL,), jnp.float32)
        inp['ln_b'] = jnp.zeros((D_MODEL,), jnp.float32)
        return inp
    _L0_attn_all = _L0_attn_setup()
    _L0_attn_in = {k: v for k, v in _L0_attn_all.items() if k in ('fw_W_in', 'fw_conv_w', 'fw_conv_b', 'fw_W_xproj', 'fw_W_dt', 'fw_b_dt', 'fw_A_log', 'fw_D_skip', 'fw_W_out', 'bw_W_in', 'bw_conv_w', 'bw_conv_b', 'bw_W_xproj', 'bw_W_dt', 'bw_b_dt', 'bw_A_log', 'bw_D_skip', 'bw_W_out', 'ln_g', 'ln_b')}
    del _L0_attn_all

    def _L0_ffn_setup():
        import jax, jax.numpy as jnp
        import numpy as np
        E, D, H = (8, 128, 512)
        B, N = (8, 128)
        key = jax.random.key(seed)
        ks = jax.random.split(key, 4)

        def init(k, shape, fan_in):
            return jax.random.normal(k, shape, jnp.float32) * (1.0 / np.sqrt(fan_in))
        return {'x': jax.random.normal(ks[0], (B, N, D), jnp.float32), 'Wr': init(ks[1], (D, E), D), 'br': jnp.zeros((E,), jnp.float32), 'W1': init(ks[2], (E, D, H), D), 'b1': jnp.zeros((E, H), jnp.float32), 'W2': init(ks[3], (E, H, D), H), 'b2': jnp.zeros((E, D), jnp.float32)}
    _L0_ffn_all = _L0_ffn_setup()
    _L0_ffn_in = {k: v for k, v in _L0_ffn_all.items() if k in ('Wr', 'br', 'W1', 'b1', 'W2', 'b2')}
    del _L0_ffn_all

    def _L1_attn_setup():
        import jax, jax.numpy as jnp
        import numpy as np
        HEADS = 8
        DIM_HEAD = 64
        MAX_FREQ = 10.0

        def _rope_tables(n):
            half = DIM_HEAD // 2
            inv_freq = 1.0 / MAX_FREQ ** (jnp.arange(0, half, 2, dtype=jnp.float32) / half)
            t = jnp.arange(n, dtype=jnp.float32)
            freqs = t[:, None] * inv_freq[None, :]
            freqs = jnp.concatenate([freqs, freqs], axis=-1)
            return (jnp.cos(freqs), jnp.sin(freqs))

        def _apply_rope(x, cos, sin):
            b, h, n, dh = x.shape
            xr = x.reshape(b, h, n, dh // 2, 2)
            x1, x2 = (xr[..., 0], xr[..., 1])
            o1 = x1 * cos - x2 * sin
            o2 = x1 * sin + x2 * cos
            return jnp.stack([o1, o2], axis=-1).reshape(b, h, n, dh)
        key = jax.random.key(seed)
        k1, k2, k3, k4, k5, k6 = jax.random.split(key, 6)
        b, n, d = (2, 1024, 128)
        inner = HEADS * DIM_HEAD
        s = lambda fan_in: 1.0 / np.sqrt(fan_in)
        return {'x': jax.random.normal(k1, (b, n, d), dtype=jnp.float32), 'w_qkv': jax.random.normal(k2, (d, 3 * inner), dtype=jnp.float32) * s(d), 'w_gates': jax.random.normal(k3, (d, HEADS), dtype=jnp.float32) * s(d), 'b_gates': jax.random.normal(k4, (HEADS,), dtype=jnp.float32) * s(d), 'w_out': jax.random.normal(k5, (inner, d), dtype=jnp.float32) * s(inner), 'b_out': jax.random.normal(k6, (d,), dtype=jnp.float32) * s(inner)}
    _L1_attn_all = _L1_attn_setup()
    _L1_attn_in = {k: v for k, v in _L1_attn_all.items() if k in ('w_qkv', 'w_gates', 'b_gates', 'w_out', 'b_out')}
    del _L1_attn_all

    def _L1_ffn_setup():
        import jax, jax.numpy as jnp
        import numpy as np
        D = 128
        E = 8
        K = 2
        EXP = 4
        LN_EPS = 1e-05
        key = jax.random.key(seed)
        ks = jax.random.split(key, 8)
        B, T = (8, 512)
        Dh = D * EXP
        x = jax.random.normal(ks[0], (B, T, D), dtype=jnp.float32)
        ln_g = jnp.ones((D,), dtype=jnp.float32)
        ln_b = jnp.zeros((D,), dtype=jnp.float32)
        lim_r = np.sqrt(6.0 / (D + E)).astype(np.float32)
        w_r = jax.random.uniform(ks[1], (E, D), dtype=jnp.float32, minval=-lim_r, maxval=lim_r)
        b_r = jnp.zeros((E,), dtype=jnp.float32)
        lim1 = np.sqrt(6.0 / (D + Dh)).astype(np.float32)
        W1 = jax.random.uniform(ks[2], (E, D, Dh), dtype=jnp.float32, minval=-lim1, maxval=lim1)
        b1 = jnp.zeros((E, Dh), dtype=jnp.float32)
        W2 = jax.random.uniform(ks[3], (E, Dh, D), dtype=jnp.float32, minval=-lim1, maxval=lim1)
        b2 = jnp.zeros((E, D), dtype=jnp.float32)
        return {'x': x, 'ln_g': ln_g, 'ln_b': ln_b, 'w_r': w_r, 'b_r': b_r, 'W1': W1, 'b1': b1, 'W2': W2, 'b2': b2}
    _L1_ffn_all = _L1_ffn_setup()
    _L1_ffn_in = {k: v for k, v in _L1_ffn_all.items() if k in ('ln_g', 'ln_b', 'w_r', 'b_r', 'W1', 'b1', 'W2', 'b2')}
    del _L1_ffn_all
    return {'x': x, 'L0_tok_W_proj': _L0_tok_in['W_proj'], 'L0_tok_b_proj': _L0_tok_in['b_proj'], 'L0_tok_W_dw': _L0_tok_in['W_dw'], 'L0_tok_b_dw': _L0_tok_in['b_dw'], 'L0_tok_W_pw': _L0_tok_in['W_pw'], 'L0_tok_b_pw': _L0_tok_in['b_pw'], 'L0_tok_gamma': _L0_tok_in['gamma'], 'L0_tok_beta': _L0_tok_in['beta'], 'L0_attn_fw_W_in': _L0_attn_in['fw_W_in'], 'L0_attn_fw_conv_w': _L0_attn_in['fw_conv_w'], 'L0_attn_fw_conv_b': _L0_attn_in['fw_conv_b'], 'L0_attn_fw_W_xproj': _L0_attn_in['fw_W_xproj'], 'L0_attn_fw_W_dt': _L0_attn_in['fw_W_dt'], 'L0_attn_fw_b_dt': _L0_attn_in['fw_b_dt'], 'L0_attn_fw_A_log': _L0_attn_in['fw_A_log'], 'L0_attn_fw_D_skip': _L0_attn_in['fw_D_skip'], 'L0_attn_fw_W_out': _L0_attn_in['fw_W_out'], 'L0_attn_bw_W_in': _L0_attn_in['bw_W_in'], 'L0_attn_bw_conv_w': _L0_attn_in['bw_conv_w'], 'L0_attn_bw_conv_b': _L0_attn_in['bw_conv_b'], 'L0_attn_bw_W_xproj': _L0_attn_in['bw_W_xproj'], 'L0_attn_bw_W_dt': _L0_attn_in['bw_W_dt'], 'L0_attn_bw_b_dt': _L0_attn_in['bw_b_dt'], 'L0_attn_bw_A_log': _L0_attn_in['bw_A_log'], 'L0_attn_bw_D_skip': _L0_attn_in['bw_D_skip'], 'L0_attn_bw_W_out': _L0_attn_in['bw_W_out'], 'L0_attn_ln_g': _L0_attn_in['ln_g'], 'L0_attn_ln_b': _L0_attn_in['ln_b'], 'L0_ffn_Wr': _L0_ffn_in['Wr'], 'L0_ffn_br': _L0_ffn_in['br'], 'L0_ffn_W1': _L0_ffn_in['W1'], 'L0_ffn_b1': _L0_ffn_in['b1'], 'L0_ffn_W2': _L0_ffn_in['W2'], 'L0_ffn_b2': _L0_ffn_in['b2'], 'L1_attn_w_qkv': _L1_attn_in['w_qkv'], 'L1_attn_w_gates': _L1_attn_in['w_gates'], 'L1_attn_b_gates': _L1_attn_in['b_gates'], 'L1_attn_w_out': _L1_attn_in['w_out'], 'L1_attn_b_out': _L1_attn_in['b_out'], 'L1_ffn_ln_g': _L1_ffn_in['ln_g'], 'L1_ffn_ln_b': _L1_ffn_in['ln_b'], 'L1_ffn_w_r': _L1_ffn_in['w_r'], 'L1_ffn_b_r': _L1_ffn_in['b_r'], 'L1_ffn_W1': _L1_ffn_in['W1'], 'L1_ffn_b1': _L1_ffn_in['b1'], 'L1_ffn_W2': _L1_ffn_in['W2'], 'L1_ffn_b2': _L1_ffn_in['b2']}

def reference(x, L0_tok_W_proj, L0_tok_b_proj, L0_tok_W_dw, L0_tok_b_dw, L0_tok_W_pw, L0_tok_b_pw, L0_tok_gamma, L0_tok_beta, L0_attn_fw_W_in, L0_attn_fw_conv_w, L0_attn_fw_conv_b, L0_attn_fw_W_xproj, L0_attn_fw_W_dt, L0_attn_fw_b_dt, L0_attn_fw_A_log, L0_attn_fw_D_skip, L0_attn_fw_W_out, L0_attn_bw_W_in, L0_attn_bw_conv_w, L0_attn_bw_conv_b, L0_attn_bw_W_xproj, L0_attn_bw_W_dt, L0_attn_bw_b_dt, L0_attn_bw_A_log, L0_attn_bw_D_skip, L0_attn_bw_W_out, L0_attn_ln_g, L0_attn_ln_b, L0_ffn_Wr, L0_ffn_br, L0_ffn_W1, L0_ffn_b1, L0_ffn_W2, L0_ffn_b2, L1_attn_w_qkv, L1_attn_w_gates, L1_attn_b_gates, L1_attn_w_out, L1_attn_b_out, L1_ffn_ln_g, L1_ffn_ln_b, L1_ffn_w_r, L1_ffn_b_r, L1_ffn_W1, L1_ffn_b1, L1_ffn_W2, L1_ffn_b2):
    import jax
    import jax.numpy as jnp

    def _L0_tok_ref(x, W_proj, b_proj, W_dw, b_dw, W_pw, b_pw, gamma, beta):
        import jax, jax.numpy as jnp
        import numpy as np
        B, C_IN, DIM, L = (8, 64, 128, 1024)

        def _layer_norm(y, gamma, beta, eps=1e-05):
            mu = jnp.mean(y, axis=-1, keepdims=True)
            var = jnp.mean(jnp.square(y - mu), axis=-1, keepdims=True)
            return (y - mu) * jax.lax.rsqrt(var + eps) * gamma + beta
        y = jnp.einsum('bcl,dc->bdl', x, W_proj) + b_proj[None, :, None]
        yp = jnp.pad(y, ((0, 0), (0, 0), (1, 1)))
        n = y.shape[-1]
        y = W_dw[None, :, 0:1] * yp[:, :, 0:n] + W_dw[None, :, 1:2] * yp[:, :, 1:n + 1] + W_dw[None, :, 2:3] * yp[:, :, 2:n + 2] + b_dw[None, :, None]
        y = jnp.einsum('bdl,ed->bel', y, W_pw) + b_pw[None, :, None]
        y = jax.nn.silu(y)
        y = jnp.transpose(y, (0, 2, 1))
        return _layer_norm(y, gamma, beta)

    def _L0_attn_ref(x, fw_W_in, fw_conv_w, fw_conv_b, fw_W_xproj, fw_W_dt, fw_b_dt, fw_A_log, fw_D_skip, fw_W_out, bw_W_in, bw_conv_w, bw_conv_b, bw_W_xproj, bw_W_dt, bw_b_dt, bw_A_log, bw_D_skip, bw_W_out, ln_g, ln_b):
        import jax, jax.numpy as jnp
        import numpy as np
        D_MODEL = 128
        D_STATE = 16
        D_CONV = 4
        D_INNER = 256
        DT_RANK = 32
        B = 2
        L = 512

        def _mamba(x, W_in, conv_w, conv_b, W_xproj, W_dt, b_dt, A_log, D_skip, W_out):
            Bb, Ll, _ = x.shape
            xz = jnp.einsum('bld,ed->ble', x, W_in)
            xc, z = jnp.split(xz, 2, axis=-1)
            xp = jnp.pad(xc, ((0, 0), (D_CONV - 1, 0), (0, 0)))
            xc = conv_b + sum((xp[:, k:k + Ll, :] * conv_w[:, k] for k in range(D_CONV)))
            xc = jax.nn.silu(xc)
            proj = jnp.einsum('bld,ed->ble', xc, W_xproj)
            dt, Bm, Cm = jnp.split(proj, [DT_RANK, DT_RANK + D_STATE], axis=-1)
            dt = jax.nn.softplus(jnp.einsum('blr,dr->bld', dt, W_dt) + b_dt)
            A = -jnp.exp(A_log)

            def step(h, inp):
                dt_t, B_t, C_t, u_t = inp
                dA = jnp.exp(dt_t[..., None] * A)
                h = dA * h + dt_t[..., None] * B_t[:, None, :] * u_t[..., None]
                y = jnp.einsum('bdn,bn->bd', h, C_t)
                return (h, y)
            h0 = jnp.zeros((Bb, D_INNER, D_STATE), x.dtype)
            _, ys = jax.lax.scan(step, h0, (dt.swapaxes(0, 1), Bm.swapaxes(0, 1), Cm.swapaxes(0, 1), xc.swapaxes(0, 1)))
            y = ys.swapaxes(0, 1) + xc * D_skip
            y = y * jax.nn.silu(z)
            return jnp.einsum('ble,de->bld', y, W_out)

        def _block(x, fw, bw, ln_g, ln_b):
            f = _mamba(x, *fw)
            b = jnp.flip(_mamba(jnp.flip(x, 1), *bw), 1)
            out = (f + b) * 0.5
            mu = out.mean(-1, keepdims=True)
            var = ((out - mu) ** 2).mean(-1, keepdims=True)
            out = (out - mu) * jax.lax.rsqrt(var + 1e-05) * ln_g + ln_b
            return jax.nn.silu(out) + x

        def _params(key, pfx):
            ks = jax.random.split(key, 5)

            def n(k, shape, fan):
                return jax.random.normal(k, shape, jnp.float32) * fan ** (-0.5)
            return {pfx + 'W_in': n(ks[0], (2 * D_INNER, D_MODEL), D_MODEL), pfx + 'conv_w': n(ks[1], (D_INNER, D_CONV), D_CONV), pfx + 'conv_b': jnp.zeros((D_INNER,), jnp.float32), pfx + 'W_xproj': n(ks[2], (DT_RANK + 2 * D_STATE, D_INNER), D_INNER), pfx + 'W_dt': n(ks[3], (D_INNER, DT_RANK), DT_RANK), pfx + 'b_dt': jnp.full((D_INNER,), -4.0, jnp.float32), pfx + 'A_log': jnp.log(jnp.tile(jnp.arange(1, D_STATE + 1, dtype=jnp.float32), (D_INNER, 1))), pfx + 'D_skip': jnp.ones((D_INNER,), jnp.float32), pfx + 'W_out': n(ks[4], (D_MODEL, D_INNER), D_INNER)}
        fw = (fw_W_in, fw_conv_w, fw_conv_b, fw_W_xproj, fw_W_dt, fw_b_dt, fw_A_log, fw_D_skip, fw_W_out)
        bw = (bw_W_in, bw_conv_w, bw_conv_b, bw_W_xproj, bw_W_dt, bw_b_dt, bw_A_log, bw_D_skip, bw_W_out)
        return _block(x, fw, bw, ln_g, ln_b)

    def _L0_ffn_ref(x, Wr, br, W1, b1, W2, b2):
        import jax, jax.numpy as jnp
        import numpy as np
        E, D, H = (8, 128, 512)
        B, N = (8, 128)
        b, n, d = x.shape
        xt = x.reshape(-1, d)
        route_prob = jax.nn.softmax(xt.astype(jnp.float32) @ Wr + br, axis=-1)
        routes = jnp.argmax(route_prob, axis=-1)
        p_max = jnp.max(route_prob, axis=-1)

        def expert_step(acc, inp):
            w1, bb1, w2, bb2, e = inp
            h = jax.nn.gelu(xt @ w1 + bb1, approximate=False)
            y = h @ w2 + bb2
            return (acc + y * (routes == e)[:, None].astype(y.dtype), None)
        out, _ = jax.lax.scan(expert_step, jnp.zeros_like(xt), (W1, b1, W2, b2, jnp.arange(E)))
        out = out * (p_max / jax.lax.stop_gradient(p_max))[:, None]
        return out.reshape(b, n, d)

    def _L1_attn_ref(x, w_qkv, w_gates, b_gates, w_out, b_out):
        import jax, jax.numpy as jnp
        import numpy as np
        HEADS = 8
        DIM_HEAD = 64
        MAX_FREQ = 10.0

        def _rope_tables(n):
            half = DIM_HEAD // 2
            inv_freq = 1.0 / MAX_FREQ ** (jnp.arange(0, half, 2, dtype=jnp.float32) / half)
            t = jnp.arange(n, dtype=jnp.float32)
            freqs = t[:, None] * inv_freq[None, :]
            freqs = jnp.concatenate([freqs, freqs], axis=-1)
            return (jnp.cos(freqs), jnp.sin(freqs))

        def _apply_rope(x, cos, sin):
            b, h, n, dh = x.shape
            xr = x.reshape(b, h, n, dh // 2, 2)
            x1, x2 = (xr[..., 0], xr[..., 1])
            o1 = x1 * cos - x2 * sin
            o2 = x1 * sin + x2 * cos
            return jnp.stack([o1, o2], axis=-1).reshape(b, h, n, dh)
        b, n, d = x.shape
        h, dh = (HEADS, DIM_HEAD)
        scale = dh ** (-0.5)
        qkv = x @ w_qkv
        q, k, v = jnp.split(qkv, 3, axis=-1)
        to_bhnd = lambda t: t.reshape(b, n, h, dh).transpose(0, 2, 1, 3)
        q, k, v = (to_bhnd(q), to_bhnd(k), to_bhnd(v))
        cos, sin = _rope_tables(n)
        q = _apply_rope(q, cos, sin)
        k = _apply_rope(k, cos, sin)
        dots = jnp.einsum('bhid,bhjd->bhij', q, k) * scale
        attn = jax.nn.softmax(dots, axis=-1)
        gates = jax.nn.sigmoid(x @ w_gates + b_gates)
        out = jnp.einsum('bhij,bhjd->bhid', attn, v)
        out = out * gates.transpose(0, 2, 1)[..., None]
        out = out.transpose(0, 2, 1, 3).reshape(b, n, h * dh)
        return out @ w_out + b_out

    def _L1_ffn_ref(x, ln_g, ln_b, w_r, b_r, W1, b1, W2, b2):
        import jax, jax.numpy as jnp
        import numpy as np
        D = 128
        E = 8
        K = 2
        EXP = 4
        LN_EPS = 1e-05
        B, T, d = x.shape
        mu = jnp.mean(x, axis=-1, keepdims=True)
        var = jnp.mean(jnp.square(x - mu), axis=-1, keepdims=True)
        h = (x - mu) * jax.lax.rsqrt(var + LN_EPS) * ln_g + ln_b
        logits = jnp.einsum('btd,ed->bte', h, w_r) + b_r
        topk_vals, topk_idx = jax.lax.top_k(logits, K)
        gates = jax.nn.softmax(topk_vals, axis=-1)
        hf = h.reshape(B * T, d)
        hid = jax.nn.gelu(jnp.einsum('nd,edf->nef', hf, W1) + b1, approximate=False)
        expert_stack = jnp.einsum('nef,efd->ned', hid, W2) + b2
        idx_flat = topk_idx.reshape(B * T, K)
        gates_flat = gates.reshape(B * T, K)
        gathered = jnp.take_along_axis(expert_stack, idx_flat[:, :, None], axis=1)
        mixed = jnp.sum(gathered * gates_flat[:, :, None], axis=1).reshape(B, T, d)
        return x + mixed
    h = _L0_tok_ref(x, L0_tok_W_proj, L0_tok_b_proj, L0_tok_W_dw, L0_tok_b_dw, L0_tok_W_pw, L0_tok_b_pw, L0_tok_gamma, L0_tok_beta)
    h = h + _L0_attn_ref(_layernorm(h, axis=-1), L0_attn_fw_W_in, L0_attn_fw_conv_w, L0_attn_fw_conv_b, L0_attn_fw_W_xproj, L0_attn_fw_W_dt, L0_attn_fw_b_dt, L0_attn_fw_A_log, L0_attn_fw_D_skip, L0_attn_fw_W_out, L0_attn_bw_W_in, L0_attn_bw_conv_w, L0_attn_bw_conv_b, L0_attn_bw_W_xproj, L0_attn_bw_W_dt, L0_attn_bw_b_dt, L0_attn_bw_A_log, L0_attn_bw_D_skip, L0_attn_bw_W_out, L0_attn_ln_g, L0_attn_ln_b)
    h = h + _L0_ffn_ref(_layernorm(h, axis=-1), L0_ffn_Wr, L0_ffn_br, L0_ffn_W1, L0_ffn_b1, L0_ffn_W2, L0_ffn_b2)
    h = h + _L1_attn_ref(_layernorm(h, axis=-1), L1_attn_w_qkv, L1_attn_w_gates, L1_attn_b_gates, L1_attn_w_out, L1_attn_b_out)
    h = h + _L1_ffn_ref(_layernorm(h, axis=-1), L1_ffn_ln_g, L1_ffn_ln_b, L1_ffn_w_r, L1_ffn_b_r, L1_ffn_W1, L1_ffn_b1, L1_ffn_W2, L1_ffn_b2)
    return h

_drawn_inputs = setup_inputs


def setup_inputs(seed=0):
    import zlib

    import numpy as np

    out = dict(_drawn_inputs(seed))
    spreads = {'L0_tok_b_proj': (0.0, 0.1),
     'L0_tok_b_dw': (0.0, 0.1),
     'L0_tok_b_pw': (0.0, 0.1),
     'L0_tok_gamma': (1.0, 0.2),
     'L0_tok_beta': (0.0, 0.1),
     'L0_attn_fw_conv_b': (0.0, 0.1),
     'L0_attn_fw_b_dt': (-4.0, 0.2),
     'L0_attn_fw_D_skip': (1.0, 0.2),
     'L0_attn_bw_conv_b': (0.0, 0.1),
     'L0_attn_bw_b_dt': (-4.0, 0.2),
     'L0_attn_bw_D_skip': (1.0, 0.2),
     'L0_attn_ln_g': (1.0, 0.2),
     'L0_attn_ln_b': (0.0, 0.1),
     'L0_ffn_br': (0.0, 0.1),
     'L0_ffn_b1': (0.0, 0.1),
     'L0_ffn_b2': (0.0, 0.1),
     'L1_ffn_ln_g': (1.0, 0.2),
     'L1_ffn_ln_b': (0.0, 0.1),
     'L1_ffn_b_r': (0.0, 0.507),
     'L1_ffn_b1': (0.0, 0.424),
     'L1_ffn_b2': (0.0, 0.335)}
    factors = {'L1_attn_w_gates': 2.949, 'L1_attn_b_gates': 29.671}
    for name, (base, spread) in spreads.items():
        noise = np.random.default_rng([zlib.crc32(name.encode()), seed]).standard_normal(out[name].shape)
        drawn = base * np.exp(spread * noise) if base else spread * noise
        out[name] = jnp.asarray(drawn.astype(out[name].dtype))
    for name, factor in factors.items():
        out[name] = (out[name] * factor).astype(out[name].dtype)
    return out
```

```python
from contextlib import ExitStack

import concourse.bass as bass
from concourse import mybir

ALU = mybir.AluOpType
ACT = mybir.ActivationFunctionType
AX_X = mybir.AxisListType.X
F32 = mybir.dt.float32
F32R = mybir.dt.float32r
U32 = mybir.dt.uint32

B, C_IN, L, D = 8, 64, 750, 128
T, NT = 125, 6
H = L // 2
D_INNER, D_STATE, D_CONV, DT_RANK = 256, 16, 4, 32
E, HID = 8, 512
HEADS, DH = 8, 64
EPS = 1e-5


class Mem:

    def __init__(self, nc, ctx, stage):
        self.nc, self.ctx, self.stage = nc, ctx, stage
        self.sems = []

    def sb(self, name, shape, dt=F32):
        return self.ctx.enter_context(self.nc.sbuf_tensor(f"{self.stage}_{name}", shape, dt))

    def ps(self, name, shape=(128, 2, 512)):
        return self.ctx.enter_context(self.nc.psum_tensor(f"{self.stage}_{name}", list(shape), F32))

    def sem(self, name):
        self.sems.append(self.ctx.enter_context(self.nc.semaphore(f"{self.stage}_{name}")))
        return self.sems[-1]

    def block(self):
        self.ctx.callback(self.clear)
        return self.ctx.enter_context(self.nc.Block())

    def clear(self):
        for s in self.sems:
            self.nc.gpsimd.sem_clear(s)
        self.nc.all_engine_barrier()


def chain(eng, sem, base):
    count = [0]

    def step(ins):
        count[0] += 1
        ins.then_inc(sem, 1)
        eng.wait_ge(sem, base + count[0])

    step.count = count
    return step


def in_pairs(eng, n=2):
    yield 0
    with eng.Fori(1, B // n) as i:
        yield i


def later(i):
    return not isinstance(i, int) or i > 0


def col(ap):
    return ap.rearrange("(p a) -> p a", a=1)


def rows(ap, n):
    return ap.rearrange("(a c) -> a c", a=1).to_broadcast([n, ap.shape[0]])


def backward(ap):
    n = ap.shape[-1]
    return bass.AP(ap.tensor, ap.offset + n - 1, [list(ap.ap[0]), [-1, n]])


def halves(ps):
    return ps[:, :, 0:H]


def split(ap):
    return ap.rearrange("p (a c) -> p a c", a=2)


def tiles3(ps):
    return ps[0:T, :, 0:3 * D]


def make_identity(nc, pool, ident, sem):
    nc.gpsimd.memset(ident[:], 0.0).then_inc(sem, 1)
    pool.wait_ge(sem, 1)
    n = ident.shape[1]
    nc.gpsimd.affine_select(out=ident[:], in_=ident[:], compare_op=ALU.not_equal, fill=1.0, base=0,
                            pattern=[[-1, n]], channel_multiplier=1).then_inc(sem, 1)


def ln_stats(nc, x, stats, mv, var_eps, step, spare):
    for k in range(NT):
        ins = nc.vector.bn_stats(stats[:, k], x[:, k])
        if k == NT - 1:
            step(ins)
    nc.vector.memset(spare, 0.0)
    for k in range(NT):
        ins = nc.vector.bn_aggr(mv[:, k], stats[:, k])
        if k == NT - 1:
            step(ins)
    return nc.vector.tensor_scalar(var_eps, mv[:, :, 1], EPS, None, ALU.add)


def ln_apply(nc, out, x, mv, rstd):
    for k in range(NT):
        ins = nc.vector.tensor_scalar(out[:, k], x[:, k], mv[:, k, 0:1], rstd[:, k:k + 1], ALU.subtract, ALU.mult)
    return ins


def stage_tok(nc, a, xln_s, res0_s):
    with ExitStack() as ctx:
        m = Mem(nc, ctx, "tok")
        w_proj, w_pw = m.sb("w_proj", [C_IN, D]), m.sb("w_pw", [D, D])
        vec = m.sb("vec", [D, 6])
        gamma, beta = m.sb("gamma", [T, D]), m.sb("beta", [T, D])
        ident = m.sb("ident", [128, 128])
        mhalf = m.sb("mhalf", [T, NT])
        spare = m.sb("spare", [T, 1])
        x = m.sb("x", [C_IN, 2, L])
        ypad = m.sb("ypad", [D, 2, L + 2])
        conv = m.sb("conv", [D, 2, L])
        act = m.sb("act", [D, 2, L])
        xt = m.sb("xt", [T, 2, NT, D])
        h0 = m.sb("h0", [T, 2, NT, D])
        xn = m.sb("xn", [T, 2, NT, D])
        res = m.sb("res", [T, 2, NT, D])
        fwd, bwd = m.sb("fwd", [D, 2, L]), m.sb("bwd", [D, 2, L])
        stats = m.sb("stats", [T, 2, 2, NT, 6])
        mv = m.sb("mv", [T, 2, 2, NT, 2])
        var_eps, rstd = m.sb("var_eps", [T, 2, 2, NT]), m.sb("rstd", [T, 2, 2, NT])
        pa = [m.ps(f"pa{s}") for s in range(2)]
        pb = [m.ps(f"pb{s}") for s in range(2)]

        w_loaded, ident_made, consts_set = m.sem("w_loaded"), m.sem("ident_made"), m.sem("consts_set")
        x_loaded = [m.sem(f"x_loaded{s}") for s in range(2)]
        proj_done, ypad_ready, conv_ready = m.sem("proj_done"), m.sem("ypad_ready"), m.sem("conv_ready")
        pw_done, act_ready, turned, xt_ready = m.sem("pw_done"), m.sem("act_ready"), m.sem("turned"), m.sem("xt_ready")
        var_ready, rstd_ready, xn_ready = m.sem("var_ready"), m.sem("rstd_ready"), m.sem("xn_ready")
        res_ready, turned_back, out_ready = m.sem("res_ready"), m.sem("turned_back"), m.sem("out_ready")
        dve_step, stored = m.sem("dve_step"), m.sem("stored")
        N_W = 8
        block = m.block()

        @block.sync
        def _(sp):
            for dst, src in ((w_proj[:], a["tok_W_projT"]), (w_pw[:], a["tok_W_pwT"]),
                             (vec[:, 0:1], col(a["tok_b_proj"])), (vec[:, 1:4], a["tok_W_dw"]),
                             (vec[:, 4:5], col(a["tok_b_dw"])), (vec[:, 5:6], col(a["tok_b_pw"])),
                             (gamma[:], rows(a["tok_gamma"], T)), (beta[:], rows(a["tok_beta"], T))):
                sp.dma_start(dst, src).then_inc(w_loaded, 16)
            for s in range(2):
                sp.dma_start(x[:, s], a["x"][s]).then_inc(x_loaded[s], 16)
            with sp.Fori(0, B // 2 - 1) as i:
                for s in range(2):
                    sp.wait_ge(proj_done, 2 * i + s + 1)
                    sp.dma_start(x[:, s], a["x"][2 * i + s + 2]).then_inc(x_loaded[s], 16)

        @block.tensor
        def _(pe):
            pe.wait_ge(w_loaded, 16 * N_W)
            pe.wait_ge(ident_made, 2)
            for i in in_pairs(pe):
                for s in range(2):
                    pe.wait_ge(x_loaded[s], 16 * i + 16)
                    if later(i):
                        pe.wait_ge(xt_ready, 2 * i)
                    for g in range(2):
                        last = nc.tensor.matmul(pa[s][:, g, 0:H], w_proj[:], x[:, s, g * H:(g + 1) * H],
                                                start=True, stop=True)
                    last.then_inc(proj_done, 1)
                for s in range(2):
                    pe.wait_ge(conv_ready, 2 * i + s + 1)
                    if later(i):
                        pe.wait_ge(out_ready, 4 * i)
                    for g in range(2):
                        last = nc.tensor.matmul(pb[s][:, g, 0:H], w_pw[:], conv[:, s, g * H:(g + 1) * H],
                                                start=True, stop=True)
                    last.then_inc(pw_done, 1)
                for s in range(2):
                    pe.wait_ge(act_ready, 2 * i + s + 1)
                    for k in range(NT):
                        last = nc.tensor.transpose(pa[s][0:T, k // 3, (k % 3) * D:(k % 3 + 1) * D],
                                                   act[:, s, k * T:(k + 1) * T], ident[:])
                    last.then_inc(turned, 1)
                for s in range(2):
                    pe.wait_ge(xn_ready, 4 * i + 2 + s + 1)
                    for k in range(NT):
                        last = nc.tensor.transpose(pb[s][:, k // 3, (k % 3) * T:(k % 3 + 1) * T],
                                                   xn[:, s, k], ident[0:T, 0:T])
                    last.then_inc(turned_back, 1)

        @block.scalar
        def _(act_e):
            act_e.wait_ge(w_loaded, 16 * N_W)
            act_e.wait_ge(consts_set, 3)
            for i in in_pairs(act_e):
                for s in range(2):
                    act_e.wait_ge(proj_done, 2 * i + s + 1)
                    if later(i):
                        act_e.wait_ge(conv_ready, 2 * i)
                    nc.scalar.activation(split(ypad[:, s, 1:L + 1]), halves(pa[s]), ACT.Identity,
                                         bias=vec[:, 0:1]).then_inc(ypad_ready, 1)
                for s in range(2):
                    act_e.wait_ge(pw_done, 2 * i + s + 1)
                    if later(i):
                        act_e.wait_ge(turned, 2 * i)
                    nc.scalar.activation(split(act[:, s]), halves(pb[s]), ACT.Silu,
                                         bias=vec[:, 5:6]).then_inc(act_ready, 1)
                for s in range(2):
                    act_e.wait_ge(turned, 2 * i + s + 1)
                    if later(i):
                        act_e.wait_ge(xn_ready, 4 * i)
                    nc.scalar.activation(xt[:, s].rearrange("p (a k) c -> p a (k c)", a=2), tiles3(pa[s]),
                                         ACT.Copy).then_inc(xt_ready, 1)
                for s in range(2):
                    act_e.wait_ge(turned_back, 2 * i + s + 1)
                    if later(i):
                        act_e.wait_ge(stored, 96 * i)
                    nc.scalar.activation(split(fwd[:, s]), halves(pb[s]), ACT.Copy).then_inc(out_ready, 1)
                    act_e.wait_ge(out_ready, 4 * i + 2 * s + 1)
                    nc.scalar.activation(bwd[:, s], backward(fwd[:, s]), ACT.Copy).then_inc(out_ready, 1)
                for s in range(2):
                    act_e.wait_ge(res_ready, 2 * i + s + 1)
                    act_e.dma_start(res0_s[2 * i + s].rearrange("(k p) c -> p k c", p=T), res[:, s]).then_inc(stored, 16)
                    act_e.wait_ge(out_ready, 4 * i + 2 * s + 2)
                    act_e.dma_start(xln_s[4 * i + 2 * s], fwd[:, s]).then_inc(stored, 16)
                    act_e.dma_start(xln_s[4 * i + 2 * s + 1], bwd[:, s]).then_inc(stored, 16)
            act_e.wait_ge(stored, 48 * B)

        @block.vector
        def _(dve):
            nc.vector.memset(ypad[:, :, 0:1], 0.0).then_inc(consts_set, 1)
            nc.vector.memset(ypad[:, :, L + 1:L + 2], 0.0).then_inc(consts_set, 1)
            nc.vector.memset(mhalf[:], -0.5).then_inc(consts_set, 1)
            dve.wait_ge(w_loaded, 16 * N_W)
            steps = 2 * (2 + 2 + 2 + 2)
            for i in in_pairs(dve):
                step = chain(dve, dve_step, i * steps)
                for s in range(2):
                    dve.wait_ge(ypad_ready, 2 * i + s + 1)
                    if later(i):
                        dve.wait_ge(pw_done, 2 * i)
                    step(nc.vector.tensor_scalar(conv[:, s], ypad[:, s, 0:L], vec[:, 1:2], vec[:, 4:5],
                                                 ALU.mult, ALU.add))
                    step(nc.vector.scalar_tensor_tensor(conv[:, s], ypad[:, s, 1:L + 1], vec[:, 2:3],
                                                        conv[:, s], ALU.mult, ALU.add))
                    nc.vector.scalar_tensor_tensor(conv[:, s], ypad[:, s, 2:L + 2], vec[:, 3:4],
                                                   conv[:, s], ALU.mult, ALU.add).then_inc(conv_ready, 1)
                for s in range(2):
                    dve.wait_ge(xt_ready, 2 * i + s + 1)
                    ln_stats(nc, xt[:, s], stats[:, s, 0], mv[:, s, 0], var_eps[:, s, 0], step, spare[:]).then_inc(var_ready, 1)
                for s in range(2):
                    dve.wait_ge(rstd_ready, 4 * i + s + 1)
                    ln_apply(nc, h0[:, s], xt[:, s], mv[:, s, 0], rstd[:, s, 0]).then_inc(xn_ready, 1)
                    dve.wait_ge(xn_ready, 4 * i + s + 1)
                    step(nc.vector.tensor_tensor(h0[:, s], h0[:, s], gamma[:].unsqueeze(1).to_broadcast([T, NT, D]), ALU.mult))
                    step(nc.vector.tensor_tensor(h0[:, s], h0[:, s], beta[:].unsqueeze(1).to_broadcast([T, NT, D]), ALU.add))
                for s in range(2):
                    ln_stats(nc, h0[:, s], stats[:, s, 1], mv[:, s, 1], var_eps[:, s, 1], step, spare[:]).then_inc(var_ready, 1)
                for s in range(2):
                    dve.wait_ge(rstd_ready, 4 * i + 2 + s + 1)
                    if later(i):
                        dve.wait_ge(turned_back, 2 * i)
                    ln_apply(nc, xn[:, s], h0[:, s], mv[:, s, 1], rstd[:, s, 1]).then_inc(xn_ready, 1)
                    dve.wait_ge(xn_ready, 4 * i + 2 + s + 1)
                    if later(i):
                        dve.wait_ge(stored, 96 * i)
                    nc.vector.tensor_tensor(res[:, s], h0[:, s], xn[:, s], ALU.add).then_inc(res_ready, 1)
                assert step.count[0] == steps

        @block.gpsimd
        def _(pool):
            make_identity(nc, pool, ident, ident_made)
            pool.wait_ge(consts_set, 3)
            for i in in_pairs(pool):
                for r in range(2):
                    for s in range(2):
                        pool.wait_ge(var_ready, 4 * i + 2 * r + s + 1)
                        nc.gpsimd.tensor_tensor(rstd[:, s, r], var_eps[:, s, r], mhalf[:], ALU.pow).then_inc(rstd_ready, 1)


def stage_mamba(nc, a, xln_s, brow_s, mix_s):
    NG = 2
    UNITS = 2 * D_STATE * NG
    SEQS = 2 * B
    BN = 4
    X_ROWS = 96
    W = H + 1
    ROWS_AT = 50
    OUT1, IN, OUT0, XP, DT = 0, tuple(range(1, 9)), 9, (10, 11), (12, 13, 14, 15)
    PRO, PER = 14, 16
    with ExitStack() as ctx:
        m = Mem(nc, ctx, "mb")
        w_in = m.sb("w_in", [D, 2, 2 * D_INNER])
        w_tap = m.sb("w_tap", [D, 2, D_CONV, D_INNER])
        w_x = m.sb("w_x", [128, 2, NG, X_ROWS])
        w_dt = m.sb("w_dt", [X_ROWS, 2, D_INNER])
        w_out = m.sb("w_out", [128, 2, NG, D])
        vec = m.sb("vec", [128, 2, 3, NG])
        a_neg = m.sb("a_neg", [128, 2, NG, D_STATE])
        ident = m.sb("ident", [128, 128])
        pick_f, pick = m.sb("pick_f", [64, D_STATE, 128]), m.sb("pick", [64, D_STATE, 128], F32R)
        PAD = D_CONV - 1
        xs = m.sb("xs", [D, 2, PAD + L])
        xcv = m.sb("xcv", [128, NG, L])
        u, sz = m.sb("u", [128, 2, NG, L]), m.sb("sz", [128, 2, NG, L])
        dt, du = m.sb("dt", [128, 2, NG, L]), m.sb("du", [128, 2, NG, L])
        vt, lt = m.sb("vt", [128, NG, L]), m.sb("lt", [128, NG, L])
        xp = m.sb("xp", [X_ROWS, L])
        bc = m.sb("bc", [64, 2, L], F32R)
        bb = m.sb("bb", [128, 4, BN, H])
        dbu = m.sb("dbu", [128, 4, H])
        hs = m.sb("hs", [128, D_STATE, NG, H])
        hc = m.sb("hc", [128, 4, H])
        yv = m.sb("yv", [128, 2, NG, H])
        ost = m.sb("ost", [D, 2, H])
        da, cb, py, pj = m.ps("da"), m.ps("cb"), m.ps("py"), m.ps("pj")

        w_loaded, a_step, picks, taps = m.sem("w_loaded"), m.sem("a_step"), m.sem("picks"), m.sem("taps")
        ident_made, pick_made, pads = m.sem("ident_made"), m.sem("pick_made"), m.sem("pads")
        x_loaded = [m.sem(f"x_loaded{d}") for d in range(2)]
        b_loaded = [m.sem(f"b_loaded{g}") for g in range(4)]
        brow_stored = m.sem("brow_stored")
        pj_done, pj_read = m.sem("pj_done"), m.sem("pj_read")
        silu_done, bc_ready, soft_step = m.sem("silu_done"), m.sem("bc_ready"), m.sem("soft_step")
        dt_ready, du_ready = m.sem("dt_ready"), m.sem("du_ready")
        da_ready, dbu_ready, scanned, cb_ready = m.sem("da_ready"), m.sem("dbu_ready"), m.sem("scanned"), m.sem("cb_ready")
        hc_ready, summed, y_read, yv_ready = m.sem("hc_ready"), m.sem("summed"), m.sem("y_read"), m.sem("yv_ready")
        stored = [m.sem(f"stored{k}") for k in range(2)]
        N_W = 2 * 7
        SOFT = 3 * NG

        def unit(j):
            k, n, c = j // (D_STATE * NG), j // NG % D_STATE, j % NG
            return k, n, c

        def bank(n_parity):
            return pj[:, n_parity, 0:H]

        def uses(q):
            return PRO - 1 + PER * q

        def run(eng, turn):
            turn(0, 0, True, True)
            with eng.Fori(0, (SEQS - 2) // 2) as i:
                turn(2 * i + 1, 1, False, True)
                turn(2 * i + 2, 0, False, True)
            turn(SEQS - 1, 1, False, False)

        IN_MM = [(t, g, k) for t in range(4) for g in range(2) for k in range(D_CONV if t < NG else 1)]
        IN_SLOT = [5 + int(1.25 * x) for x in range(len(IN_MM))]
        IN_EV = [IN_SLOT[max(x for x, (tt, gg, _) in enumerate(IN_MM) if (tt, gg) == (t, g))] + 5
                 for t in range(4) for g in range(2)]

        block = m.block()

        @block.sync
        def _(sp):
            def load_x(s, d):
                sp.dma_start(xs[:, d, PAD:], xln_s[s]).then_inc(x_loaded[d], 16)

            for d, w in enumerate(("fw_", "bw_")):
                for dst, src in ((w_in[:, d], a[w + "W_inT"]),
                                 (w_tap[:, d], a[w + "conv_wT"].rearrange("(a k) c -> a k c", a=1).to_broadcast([D, D_CONV, D_INNER])),
                                 (w_x[:, d], a[w + "W_xprojT"].rearrange("(c p) r -> p c r", c=NG)),
                                 (w_dt[64:96, d], a[w + "W_dtT"]),
                                 (w_out[:, d], a[w + "W_outT"].rearrange("(c p) r -> p c r", c=NG)),
                                 (a_neg[:, d], a[w + "A_log"].rearrange("(c p) r -> p c r", c=NG)),
                                 (vec[:, d], a[w + "vec"])):
                    sp.dma_start(dst, src).then_inc(w_loaded, 16)
                if d == 0:
                    load_x(0, 0)

            def load_b(e, g):
                k, n0 = g // 4, g % 4 * BN
                src = brow_s[e][n0:n0 + BN, k * H:(k + 1) * H]
                src = bass.AP(src.tensor, src.offset, [[0, 128]] + [list(x) for x in src.ap])
                sp.dma_start(bb[:, g % 4], src).then_inc(b_loaded[g % 4], 16)

            def store_rows(f, e, read):
                sp.wait_ge(pj_read, read)
                sp.dma_start(brow_s[e], xp[0:D_STATE, :]).then_inc(brow_stored, 16)

            store_rows(0, 0, 10)
            sp.wait_ge(brow_stored, 16)
            for g in range(4):
                load_b(0, g)

            def turn(q, d, first, more):
                if more:
                    if not first:
                        sp.wait_ge(pj_done, PER * q - 8)
                    load_x(q + 1, 1 - d)
                for g in range(4, 8):
                    sp.wait_ge(dbu_ready, UNITS * q + (g - 3) * BN * NG)
                    load_b(d, g)
                if more:
                    store_rows(q + 1, 1 - d, uses(q) + XP[1] + 1)
                    for g in range(4):
                        sp.wait_ge(dbu_ready, UNITS * q + max((g + 5) * BN * NG, ROWS_AT + 1))
                        load_b(1 - d, g)

            run(sp, turn)

        @block.tensor
        def _(pe):
            pe.wait_ge(w_loaded, 16 * N_W)
            pe.wait_ge(ident_made, 2)
            pe.wait_ge(picks, 1)
            pe.wait_ge(taps, D_CONV * 2)
            pe.wait_ge(pads, 1)

            def free(n):
                if not (isinstance(n, int) and n < 2):
                    pe.wait_ge(pj_read, n - 1)

            def proj_in(base, par, e, x):
                t, g, k = IN_MM[x]
                at = 2 * t + g
                out = bank((par + at) % 2)
                if k == 0:
                    free(base + at)
                if t < NG:
                    ins = nc.tensor.matmul(out, w_tap[:, e, k, t * 128:(t + 1) * 128], xs[:, e, g * H + k:g * H + k + H],
                                           start=(k == 0), stop=(k == D_CONV - 1))
                else:
                    ins = nc.tensor.matmul(out, w_in[:, e, t * 128:(t + 1) * 128],
                                           xs[:, e, PAD + g * H:PAD + (g + 1) * H], start=True, stop=True)
                if t >= NG or k == D_CONV - 1:
                    ins.then_inc(pj_done, 1)

            def proj_x(n, par, f, e, g):
                if g == 0:
                    pe.wait_ge(silu_done, 4 * f + 2)
                free(n)
                for c in range(NG):
                    last = nc.tensor.matmul(pj[0:X_ROWS, par, 0:H], w_x[:, e, c], u[:, e, c, g * H:(g + 1) * H],
                                            start=(c == 0), stop=(c == NG - 1))
                last.then_inc(pj_done, 1)

            def proj_dt(n, par, e, c, g):
                free(n)
                nc.tensor.matmul(bank(par), w_dt[64:96, e, c * 128:(c + 1) * 128], xp[64:96, g * H:(g + 1) * H],
                                 start=True, stop=True).then_inc(pj_done, 1)

            def proj_out(n, par, s, d, k):
                pe.wait_ge(yv_ready, 4 * s + 2 * k + 2)
                free(n)
                for c in range(NG):
                    last = nc.tensor.matmul(bank(par), w_out[:, d, c], yv[:, k, c], start=(c == 0), stop=(c == NG - 1))
                last.then_inc(pj_done, 1)

            pe.wait_ge(x_loaded[0], 16)
            for x in range(len(IN_MM)):
                proj_in(0, 0, 0, x)
            for g in range(2):
                proj_x(8 + g, g, 0, 0, g)
            pe.wait_ge(pj_read, 10)
            for c in range(NG):
                for g in range(2):
                    proj_dt(10 + 2 * c + g, g, 0, c, g)

            def turn(q, d, first, more):
                base = uses(q)
                f, e = q + 1, 1 - d
                steps = {}

                def at(slot, step):
                    steps.setdefault(slot, []).append(step)

                if not first:
                    at(3, lambda: proj_out(base, 1, q - 1, e, 1))
                if more:
                    for x, slot in enumerate(IN_SLOT):
                        if x == 0:
                            at(slot, lambda: pe.wait_ge(x_loaded[e], 8 * q + (24 if d else 16)))
                        at(slot, lambda x=x: proj_in(base + IN[0], 0, e, x))
                    for g in range(2):
                        at(39 + g, lambda g=g: proj_x(base + XP[g], (XP[g] + 1) % 2, f, e, g))
                    for h, slot in enumerate((45, 46, 50, 51)):
                        if h == 0:
                            at(slot, lambda: pe.wait_ge(pj_read, base + XP[1] + 1))
                        at(slot, lambda h=h: proj_dt(base + DT[h], (DT[h] + 1) % 2, e, h // 2, h % 2))
                out0 = OUT0 if more else 1
                at(38, lambda: proj_out(base + out0, (out0 + 1) % 2, q, d, 0))
                pe.wait_ge(bc_ready, 2 * q + 2)

                def c_rows(r):
                    k, n = r // D_STATE, r % D_STATE
                    if not (first and r < 2):
                        pe.wait_ge(hc_ready, UNITS * q + 2 * r - 2)
                    nc.tensor.matmul(cb[:, r % 2, 0:W], pick[:, n], bc[:, d, k * (L - W):k * (L - W) + W],
                                     start=True, stop=True).then_inc(cb_ready, 1)

                c_rows(0)
                for j in range(UNITS):
                    k, n, c = unit(j)
                    if c == 0 and j // 2 + 1 < UNITS // 2:
                        c_rows(j // 2 + 1)
                    if n == 0 and not (first and k == 0):
                        pe.wait_ge(y_read, 4 * q + 2 * k - 1 + c)
                    pe.wait_ge(hc_ready, UNITS * q + j + 1)
                    nc.tensor.matmul(py[:, c, 0:H], ident[:], hc[:, j % 4], start=(n == 0),
                                     stop=(n == D_STATE - 1)).then_inc(summed, 1)
                    for step in steps.get(j, []):
                        step()
                if not more:
                    proj_out(base + 2, 1, q, d, 1)

            run(pe, turn)

        @block.scalar
        def _(act):
            act.wait_ge(w_loaded, 16 * N_W)
            nc.scalar.activation(a_neg[:], a_neg[:], ACT.Exp).then_inc(a_step, 1)

            def ev_in(n, par, e, at):
                t, g = at // 2, at % 2
                cols = slice(g * H, (g + 1) * H)
                act.wait_ge(pj_done, n + 1)
                if t < NG:
                    nc.scalar.activation(xcv[:, t, cols], bank(par), ACT.Identity,
                                         bias=vec[:, e, 0, t:t + 1]).then_inc(pj_read, 1)
                else:
                    nc.scalar.activation(sz[:, e, t - NG, cols], bank(par), ACT.Copy).then_inc(pj_read, 1)

            def silus(f, e, read):
                act.wait_ge(pj_read, read)
                for c in range(NG):
                    nc.scalar.activation(u[:, e, c], xcv[:, c], ACT.Silu).then_inc(silu_done, 1)
                for c in range(NG):
                    nc.scalar.activation(sz[:, e, c], sz[:, e, c], ACT.Silu).then_inc(silu_done, 1)

            def ev_x(n, par, g):
                act.wait_ge(pj_done, n + 1)
                nc.scalar.activation(xp[:, g * H:(g + 1) * H], pj[0:X_ROWS, par, 0:H], ACT.Copy).then_inc(pj_read, 1)

            def soft_v(n, par, e, c, g):
                act.wait_ge(pj_done, n + 1)
                nc.scalar.activation(vt[:, c, g * H:(g + 1) * H], bank(par), ACT.Identity,
                                     bias=vec[:, e, 1, c:c + 1]).then_inc(pj_read, 1)

            def soft(f, c, i, read):
                count = SOFT * f + 3 * c
                if i == 0:
                    act.wait_ge(pj_read, read)
                    nc.scalar.activation(lt[:, c], vt[:, c], ACT.Abs).then_inc(soft_step, 1)
                elif i == 1:
                    act.wait_ge(soft_step, count + 1)
                    nc.scalar.activation(lt[:, c], lt[:, c], ACT.Exp, scale=-1.0).then_inc(soft_step, 1)
                else:
                    act.wait_ge(soft_step, count + 2)
                    nc.scalar.activation(lt[:, c], lt[:, c], ACT.Ln, bias=1.0).then_inc(soft_step, 1)

            def ev_out(n, par, s, k):
                act.wait_ge(pj_done, n + 1)
                if not (isinstance(s, int) and s == 0):
                    act.wait_ge(stored[k], 16 * s)
                nc.scalar.activation(ost[:, k], bank(par), ACT.Copy).then_inc(pj_read, 1)
                act.wait_ge(pj_read, n + 1)
                act.dma_start(mix_s[s][:, k * H:(k + 1) * H], ost[:, k]).then_inc(stored[k], 16)

            for at in range(8):
                ev_in(at, at % 2, 0, at)
            silus(0, 0, 8)
            nc.scalar.preload_act_table_set("natural_log_exp_and_others")
            for g in range(2):
                ev_x(8 + g, g, g)
            for c in range(NG):
                for g in range(2):
                    soft_v(10 + 2 * c + g, g, 0, c, g)
                for i in range(3):
                    soft(0, c, i, 12 + 2 * c)
            act.wait_ge(a_step, 2)

            def turn(q, d, first, more):
                base = uses(q)
                f, e = q + 1, 1 - d
                steps = {}

                def at(slot, step):
                    steps.setdefault(slot, []).append(step)

                if not first:
                    at(8, lambda: ev_out(base, 1, q - 1, 1))
                if more:
                    for x, slot in enumerate(IN_EV):
                        at(slot, lambda x=x: ev_in(base + IN[x], x % 2, e, x))
                    if not first:
                        at(IN_EV[0] - 1, lambda: act.wait_ge(yv_ready, 4 * q))
                    at(36, lambda: silus(f, e, base + OUT0))
                    at(36, lambda: nc.scalar.preload_act_table_set("natural_log_exp_and_others"))
                    at(43, lambda: act.wait_ge(bc_ready, 2 * f))
                    at(43, lambda: act.wait_ge(brow_stored, 16 * f))
                    for g in range(2):
                        at(43 + g, lambda g=g: ev_x(base + XP[g], (XP[g] + 1) % 2, g))
                    at(50, lambda: act.wait_ge(dt_ready, 2 * f))
                    for h, slot in enumerate((50, 51, 55, 56)):
                        at(slot, lambda h=h: soft_v(base + DT[h], (DT[h] + 1) % 2, e, h // 2, h % 2))
                    for c, slots in enumerate(((52, 53, 54), (57, 59, 61))):
                        for i, slot in enumerate(slots):
                            at(slot, lambda c=c, i=i: soft(f, c, i, base + DT[2 * c + 1] + 1))
                out0 = OUT0 if more else 1
                at(42, lambda: ev_out(base + out0, (out0 + 1) % 2, q, 0))
                act.wait_ge(dt_ready, 2 * q + 2)
                for j in range(UNITS):
                    k, n, c = unit(j)
                    if not (first and j < 2):
                        act.wait_ge(scanned, UNITS * q + j - 1)
                    nc.scalar.activation(da[:, j % 2, 0:H], dt[:, d, c, k * H:(k + 1) * H], ACT.Exp,
                                         scale=a_neg[:, d, c, n:n + 1]).then_inc(da_ready, 1)
                    for step in steps.get(j, []):
                        step()
                if not more:
                    ev_out(base + 2, 1, q, 1)

            run(act, turn)
            for k in range(2):
                act.wait_ge(stored[k], 16 * SEQS)

        @block.gpsimd
        def _(pool):
            make_identity(nc, pool, ident, ident_made)
            nc.gpsimd.memset(pick_f[:], 0.0).then_inc(pick_made, 1)
            pool.wait_ge(pick_made, 1)
            for r, base in enumerate((-D_STATE, -D_STATE - 32)):
                nc.gpsimd.affine_select(out=pick_f[:], in_=pick_f[:], compare_op=ALU.not_equal, fill=1.0,
                                        base=base, pattern=[[-1, D_STATE], [0, 128]],
                                        channel_multiplier=1).then_inc(pick_made, 1)
                pool.wait_ge(pick_made, r + 2)

            def turn(q, d, first, more):
                pool.wait_ge(du_ready, 2 * q + 2)
                for j in range(UNITS):
                    k, n, c = unit(j)
                    g = k * 4 + n // BN
                    if j % (BN * NG) == 0:
                        pool.wait_ge(b_loaded[g % 4], 32 * q + 16 * (k + 1))
                    if more and j == ROWS_AT:
                        pool.wait_ge(brow_stored, 16 * q + 32)
                    if not (first and j < 4):
                        pool.wait_ge(scanned, UNITS * q + j - 3)
                    nc.gpsimd.tensor_tensor(dbu[:, j % 4], du[:, d, c, k * H:(k + 1) * H],
                                            bb[:, g % 4, n % BN], ALU.mult).then_inc(dbu_ready, 1)

            run(pool, turn)

        @block.vector
        def _(dve):
            nc.vector.memset(xs[:, :, 0:PAD], 0.0).then_inc(pads, 1)
            dve.wait_ge(w_loaded, 16 * N_W)
            for d in range(2):
                for k in range(D_CONV):
                    nc.vector.tensor_tensor(w_tap[:, d, k], w_in[:, d, 0:D_INNER], w_tap[:, d, k], ALU.mult).then_inc(taps, 1)
            dve.wait_ge(pick_made, 3)
            nc.vector.tensor_copy(pick[:], pick_f[:]).then_inc(picks, 1)
            dve.wait_ge(a_step, 1)
            nc.vector.tensor_scalar(a_neg[:], a_neg[:], -1.0, None, ALU.mult).then_inc(a_step, 1)

            def split_bc(f, e, read):
                dve.wait_ge(pj_read, read)
                if not (isinstance(f, int) and f < 2):
                    dve.wait_ge(cb_ready, UNITS // 2 * (f - 1))
                nc.vector.tensor_copy(bc[:, e], xp[0:64]).then_inc(bc_ready, 1)
                dve.wait_ge(bc_ready, 2 * f + 1)
                nc.vector.tensor_tensor(bc[32:64, e], xp[32:64], bc[32:64, e], ALU.subtract).then_inc(bc_ready, 1)

            def finish_dt(f, e, c, part):
                if part == 0:
                    dve.wait_ge(soft_step, SOFT * f + 3 * c + 3)
                    nc.vector.scalar_tensor_tensor(dt[:, e, c], vt[:, c], 0.0, lt[:, c], ALU.max, ALU.add).then_inc(dt_ready, 1)
                else:
                    dve.wait_ge(dt_ready, 2 * f + c + 1)
                    nc.vector.tensor_tensor(du[:, e, c], dt[:, e, c], u[:, e, c], ALU.mult).then_inc(du_ready, 1)

            split_bc(0, 0, 10)
            for c in range(NG):
                for part in range(2):
                    finish_dt(0, 0, c, part)

            def finish_y(s, d, k):
                for c in range(NG):
                    dve.wait_ge(summed, UNITS * s + (k + 1) * UNITS // 2 - 1 + c)
                    nc.vector.scalar_tensor_tensor(yv[:, k, c], u[:, d, c, k * H:(k + 1) * H], vec[:, d, 2, c:c + 1],
                                                   py[:, c, 0:H], ALU.mult, ALU.add).then_inc(y_read, 1)
                for c in range(NG):
                    dve.wait_ge(y_read, 4 * s + 2 * k + c + 1)
                    nc.vector.tensor_tensor(yv[:, k, c], yv[:, k, c], sz[:, d, c, k * H:(k + 1) * H],
                                            ALU.mult).then_inc(yv_ready, 1)

            def turn(q, d, first, more):
                f, e = q + 1, 1 - d
                steps = {}

                def at(slot, step):
                    steps.setdefault(slot, []).append(step)

                if not first:
                    at(3, lambda: finish_y(q - 1, e, 1))
                at(37, lambda: finish_y(q, d, 0))
                if more:
                    at(45, lambda: split_bc(f, e, uses(q) + XP[1] + 1))
                    for c, slots in enumerate(((55, 56), (61, 62))):
                        for part, slot in enumerate(slots):
                            at(slot, lambda c=c, part=part: finish_dt(f, e, c, part))

                def times_c(j):
                    k, n, c = unit(j)
                    if c == 0:
                        dve.wait_ge(cb_ready, UNITS // 2 * q + j // 2 + 1)
                    if not (first and j < 4):
                        dve.wait_ge(summed, UNITS * q + j - 3)
                    dve.wait_ge(scanned, UNITS * q + j + 1)
                    nc.vector.tensor_tensor(hc[:, j % 4], hs[:, n, c], cb[:, j // 2 % 2, k:k + H], ALU.mult).then_inc(hc_ready, 1)

                for j in range(UNITS):
                    k, n, c = unit(j)
                    for step in steps.get(j, []):
                        step()
                    dve.wait_ge(dbu_ready, UNITS * q + j + 1)
                    dve.wait_ge(da_ready, UNITS * q + j + 1)
                    nc.vector.tensor_tensor_scan(hs[:, n, c], da[:, j % 2, 0:H], dbu[:, j % 4],
                                                 0.0 if k == 0 else hs[:, n, c, H - 1:H],
                                                 ALU.mult, ALU.add).then_inc(scanned, 1)
                    if j:
                        times_c(j - 1)
                times_c(UNITS - 1)
                if not more:
                    finish_y(q, d, 1)

            run(dve, turn)


def stage_norm(nc, a, stage, h_in, xT_s, res_s, mixed=None, affine=None):
    with ExitStack() as ctx:
        m = Mem(nc, ctx, stage)
        S = 4
        LN = 1 + (mixed is not None or affine is not None)
        ident = m.sb("ident", [128, 128])
        mhalf = m.sb("mhalf", [T, NT])
        spare = m.sb("spare", [T, 1])
        vec = m.sb("vec", [D, 2])
        gamma, beta = m.sb("gamma", [T, D]), m.sb("beta", [T, D])
        h = m.sb("h", [T, S, NT, D])
        fb = m.sb("fb", [D, S, 2, L])
        both = m.sb("both", [D, S, L])
        xt = m.sb("xt", [T, S, NT, D])
        g = m.sb("g", [T, S, NT, D])
        xn = m.sb("xn", [T, S, NT, D])
        xT = m.sb("xT", [D, S, L])
        stats = m.sb("stats", [T, S, 2, NT, 6])
        mv = m.sb("mv", [T, S, 2, NT, 2])
        var_eps, rstd = m.sb("var_eps", [T, S, 2, NT]), m.sb("rstd", [T, S, 2, NT])
        pa = [m.ps(f"pa{s}") for s in range(2)]
        pb = [m.ps(f"pb{s}") for s in range(2)]

        w_loaded, ident_made, consts_set = m.sem("w_loaded"), m.sem("ident_made"), m.sem("consts_set")
        h_loaded = [m.sem(f"h_loaded{s}") for s in range(S)]
        fb_loaded = [m.sem(f"fb_loaded{s}") for s in range(S)]
        both_ready, turned, xt_ready, g_ready = m.sem("both_ready"), m.sem("turned"), m.sem("xt_ready"), m.sem("g_ready")
        silu_ready, h_ready = m.sem("silu_ready"), m.sem("h_ready")
        var_ready, rstd_ready, xn_ready = m.sem("var_ready"), m.sem("rstd_ready"), m.sem("xn_ready")
        turned_back, xT_ready, res_ready = m.sem("turned_back"), m.sem("xT_ready"), m.sem("res_ready")
        dve_step, stored = m.sem("dve_step"), m.sem("stored")
        N_W = 2 * (mixed is not None or affine is not None)

        def tiles(ap):
            return ap.rearrange("(k p) c -> p k c", p=T)

        block = m.block()

        @block.sync
        def _(sp):
            if mixed is not None:
                sp.dma_start(gamma[:], rows(a["attn_ln_g"], T)).then_inc(w_loaded, 16)
                sp.dma_start(beta[:], rows(a["attn_ln_b"], T)).then_inc(w_loaded, 16)
            if affine is not None:
                sp.dma_start(vec[:, 0:1], col(affine[0])).then_inc(w_loaded, 16)
                sp.dma_start(vec[:, 1:2], col(affine[1])).then_inc(w_loaded, 16)
            for i in in_pairs(sp, S):
                for s in range(S):
                    if mixed is not None:
                        if later(i):
                            sp.wait_ge(both_ready, S * i)
                        for d in range(2):
                            sp.dma_start(fb[:, s, d], mixed[2 * S * i + 2 * s + d]).then_inc(fb_loaded[s], 16)
                    if later(i):
                        sp.wait_ge(stored, 32 * S * i)
                    sp.dma_start(h[:, s], tiles(h_in[S * i + s])).then_inc(h_loaded[s], 16)

        @block.tensor
        def _(pe):
            pe.wait_ge(ident_made, 2)
            for i in in_pairs(pe, S):
                for s in range(S):
                    if mixed is None:
                        break
                    pe.wait_ge(both_ready, S * i + s + 1)
                    if later(i) or s >= 2:
                        pe.wait_ge(xt_ready, S * i + s - 1)
                    for k in range(NT):
                        last = nc.tensor.transpose(pa[s % 2][0:T, k // 3, (k % 3) * D:(k % 3 + 1) * D],
                                                   both[:, s, k * T:(k + 1) * T], ident[:])
                    last.then_inc(turned, 1)
                for s in range(S):
                    pe.wait_ge(xn_ready, S * LN * i + S * (LN - 1) + s + 1)
                    if later(i) or s >= 2:
                        pe.wait_ge(xT_ready, S * i + s - 1)
                    for k in range(NT):
                        last = nc.tensor.transpose(pb[s % 2][:, k // 3, (k % 3) * T:(k % 3 + 1) * T],
                                                   xn[:, s, k], ident[0:T, 0:T])
                    last.then_inc(turned_back, 1)

        @block.scalar
        def _(act):
            if N_W:
                act.wait_ge(w_loaded, 16 * N_W)
            for i in in_pairs(act, S):
                for s in range(S):
                    if mixed is None:
                        break
                    act.wait_ge(turned, S * i + s + 1)
                    if later(i):
                        act.wait_ge(g_ready, S * i)
                    nc.scalar.activation(xt[:, s].rearrange("p (a k) c -> p a (k c)", a=2), tiles3(pa[s % 2]),
                                         ACT.Copy, scale=0.5).then_inc(xt_ready, 1)
                for s in range(S):
                    if mixed is None:
                        break
                    act.wait_ge(g_ready, S * i + s + 1)
                    nc.scalar.activation(g[:, s], g[:, s], ACT.Silu).then_inc(silu_ready, 1)
                for s in range(S):
                    act.wait_ge(turned_back, S * i + s + 1)
                    if later(i):
                        act.wait_ge(stored, 32 * S * i)
                    if affine is None:
                        ins = nc.scalar.activation(split(xT[:, s]), halves(pb[s % 2]), ACT.Copy)
                    else:
                        ins = nc.scalar.activation(split(xT[:, s]), halves(pb[s % 2]), ACT.Identity,
                                                   scale=vec[:, 0:1], bias=vec[:, 1:2])
                    ins.then_inc(xT_ready, 1)
                for s in range(S):
                    act.wait_ge(xT_ready, S * i + s + 1)
                    act.dma_start(tiles(res_s[S * i + s]), h[:, s]).then_inc(stored, 16)
                    act.dma_start(xT_s[S * i + s], xT[:, s]).then_inc(stored, 16)
            act.wait_ge(stored, 32 * B)

        @block.vector
        def _(dve):
            nc.vector.memset(mhalf[:], -0.5).then_inc(consts_set, 1)
            if N_W:
                dve.wait_ge(w_loaded, 16 * N_W)
            per = 2 * LN + 2 * (mixed is not None)
            wide = [T, NT, D]
            for i in in_pairs(dve, S):
                step = chain(dve, dve_step, S * per * i)
                first = 0
                if mixed is not None:
                    first = 1
                    for s in range(S):
                        dve.wait_ge(fb_loaded[s], 32 * i + 32)
                        if later(i):
                            dve.wait_ge(turned, S * i)
                        nc.vector.tensor_tensor(both[:, s], fb[:, s, 0], backward(fb[:, s, 1]), ALU.add).then_inc(both_ready, 1)
                    for s in range(S):
                        dve.wait_ge(xt_ready, S * i + s + 1)
                        ln_stats(nc, xt[:, s], stats[:, s, 0], mv[:, s, 0], var_eps[:, s, 0], step, spare[:]).then_inc(var_ready, 1)
                    for s in range(S):
                        dve.wait_ge(rstd_ready, S * LN * i + s + 1)
                        ln_apply(nc, g[:, s], xt[:, s], mv[:, s, 0], rstd[:, s, 0]).then_inc(xn_ready, 1)
                        dve.wait_ge(xn_ready, S * LN * i + s + 1)
                        step(nc.vector.tensor_tensor(g[:, s], g[:, s], gamma[:].unsqueeze(1).to_broadcast(wide), ALU.mult))
                        nc.vector.tensor_tensor(g[:, s], g[:, s], beta[:].unsqueeze(1).to_broadcast(wide), ALU.add).then_inc(g_ready, 1)
                    for s in range(S):
                        dve.wait_ge(silu_ready, S * i + s + 1)
                        dve.wait_ge(h_loaded[s], 16 * i + 16)
                        step(nc.vector.tensor_tensor(h[:, s], h[:, s], g[:, s], ALU.add))
                for r in range(first, LN):
                    again = r > first
                    x = g if again else h
                    for s in range(S):
                        dve.wait_ge(h_loaded[s], 16 * i + 16)
                        ln_stats(nc, x[:, s], stats[:, s, r], mv[:, s, r], var_eps[:, s, r], step, spare[:]).then_inc(var_ready, 1)
                    for s in range(S):
                        dve.wait_ge(rstd_ready, S * LN * i + S * r + s + 1)
                        if later(i):
                            dve.wait_ge(turned_back, S * i)
                        out = xn if r == LN - 1 else g
                        ln_apply(nc, out[:, s], x[:, s], mv[:, s, r], rstd[:, s, r]).then_inc(xn_ready, 1)
                        dve.wait_ge(xn_ready, S * LN * i + S * r + s + 1)
                        if r < LN - 1:
                            nc.vector.tensor_tensor(h[:, s], h[:, s], g[:, s], ALU.add).then_inc(res_ready, 1)
                            dve.wait_ge(res_ready, S * i + s + 1)
                assert step.count[0] == S * per

        @block.gpsimd
        def _(pool):
            make_identity(nc, pool, ident, ident_made)
            pool.wait_ge(consts_set, 1)
            for i in in_pairs(pool, S):
                for r in range(LN):
                    for s in range(S):
                        pool.wait_ge(var_ready, S * LN * i + S * r + s + 1)
                        nc.gpsimd.tensor_tensor(rstd[:, s, r], var_eps[:, s, r], mhalf[:], ALU.pow).then_inc(rstd_ready, 1)


def stage_ffn(nc, a, stage, top, xT_s, res_s, out):
    J = HID // 128
    UNITS, LAG = E * J, 3
    W = H + 1
    LO = 32
    p = stage + "_"
    with ExitStack() as ctx:
        m = Mem(nc, ctx, stage)
        w1, w2 = m.sb("w1", [D, E, HID]), m.sb("w2", [128, E, HID])
        w1r, w2r = m.sb("w1r", [D, 2, E, HID], F32R), m.sb("w2r", [128, 2, E, HID], F32R)
        b1, b2 = m.sb("b1", [128, E, J]), m.sb("b2", [E, D])
        wr, br = m.sb("wr", [D, E]), m.sb("br", [T, E])
        ident = m.sb("ident", [128, 128])
        pick_f, pick = m.sb("pick_f", [LO + E, E, 128]), m.sb("pick", [LO + E, E, 128], F32R)
        iota_i, iota = m.sb("iota_i", [T, E], mybir.dt.int32), m.sb("iota", [T, E])
        zero = m.sb("zero", [D, 1])
        xT, xr = m.sb("xT", [D, L]), m.sb("xr", [D, 2, 2, L], F32R)
        res = m.sb("res", [T, 2, NT, D])
        lg, best = m.sb("lg", [T, NT, E]), m.sb("best", [T, NT, 8])
        place, placef = m.sb("place", [T, NT, 8], U32), m.sb("placef", [T, NT, 8])
        gate, mask = m.sb("gate", [T, 2, NT]), m.sb("mask", [T, 2, NT, E])
        w = m.sb("w", [T, NT, E])
        wT, wTr = m.sb("wT", [E, 2, L]), m.sb("wTr", [LO + E, 2, L], F32R)
        wide_w = m.sb("wide_w", [128, 2, L])
        raw, scaled = m.sb("raw", [128, 2, L]), m.sb("scaled", [128, 2, L])
        hi, lo = m.sb("hi", [128, LAG + 1, L], F32R), m.sb("lo", [128, LAG + 1, L], F32R)
        yT = m.sb("yT", [D, L])
        up = [m.ps(f"up{s}") for s in range(2)]
        y = m.ps("y")
        sm = m.ps("sm")

        s_loaded, w1_loaded, w2_loaded = m.sem("s_loaded"), [m.sem(f"w1_{e}") for e in range(E)], [m.sem(f"w2_{e}") for e in range(E)]
        whi_ready, wlo_ready = m.sem("whi_ready"), m.sem("wlo_ready")
        ident_made, iota_made, pick_made, zeroed = m.sem("ident_made"), m.sem("iota_made"), m.sem("pick_made"), m.sem("zeroed")
        x_loaded, x_split = m.sem("x_loaded"), m.sem("x_split")
        res_loaded = [m.sem(f"res_loaded{s}") for s in range(2)]
        sm_done, sm_read = m.sem("sm_done"), m.sem("sm_read")
        lg_ready, gap_ready, exp_ready, w_ready = m.sem("lg_ready"), m.sem("gap_ready"), m.sem("exp_ready"), m.sem("w_ready")
        wTr_ready, dve_step = m.sem("wTr_ready"), m.sem("dve_step")
        up_done, raw_ready, scaled_ready = m.sem("up_done"), m.sem("raw_ready"), m.sem("scaled_ready")
        hi_ready, lo_ready, down_done = m.sem("hi_ready"), m.sem("lo_ready"), m.sem("down_done")
        y_read, res_done, stored = m.sem("y_read"), m.sem("res_done"), m.sem("stored")
        lo_by_pool = m.sem("lo_by_pool")
        N_S = 4

        def lo_made(eng, q, u):
            if u % 2:
                eng.wait_ge(lo_by_pool, UNITS // 2 * q + u // 2 + 1)
            else:
                eng.wait_ge(lo_ready, UNITS // 2 * q + u // 2 + 1)

        USES = (("b", 1, 1), ("b", 2, 5), ("y", 0, 7), ("b", 3, 9), ("l", 0, 11), ("b", 4, 13), ("b", 5, 17),
                ("t", 0, 19), ("b", 6, 21), ("t", 1, 23), ("b", 7, 25), ("b", 0, 29))
        PRO, PER = 4, len(USES)

        def turn_uses(q, first, more):
            kept = [x for x in USES if not (first and x[0] == "y") and (more or x[0] in "yb" and x[:2] != ("b", 0))]
            start = PRO if first else PRO - 1 + PER * q
            return [(kind, n, slot, start + i) for i, (kind, n, slot) in enumerate(kept)]

        def run(eng, turn):
            turn(0, 0, True, True)
            with eng.Fori(0, (B - 2) // 2) as i:
                turn(2 * i + 1, 1, False, True)
                turn(2 * i + 2, 0, False, True)
            turn(B - 1, 1, False, False)

        def two(ps):
            return bass.AP(ps, 0, [[1024, 128], [513, 2], [1, H]])

        def cols(g):
            return slice(g * (L - W), g * (L - W) + W)

        PASSES = ((0, 0), (1, 0), (0, 1))

        block = m.block()

        @block.sync
        def _(sp):
            def tiles(ap):
                return ap.rearrange("(k p) c -> p k c", p=T)

            def load_x(s):
                sp.dma_start(xT[:], xT_s[s]).then_inc(x_loaded, 16)

            def load_res(s, par):
                sp.dma_start(res[:, par], tiles(res_s[s])).then_inc(res_loaded[par], 16)

            def store(s, par, count):
                sp.wait_ge(res_done, count)
                sp.dma_start(tiles(out[s]), res[:, par]).then_inc(stored, 16)

            load_x(0)
            for dst, src in ((wr[:], a[p + "Wr"]), (br[:], rows(a[p + "br"], T)), (b2[:], a[p + "b2"]), (b1[:], a[p + "b1"])):
                sp.dma_start(dst, src).then_inc(s_loaded, 16)
            for e in range(E):
                sp.dma_start(w1[:, e], a[p + "W1"][:, e]).then_inc(w1_loaded[e], 16)
                sp.dma_start(w2[:, e], a[p + "W2"][:, e]).then_inc(w2_loaded[e], 16)
            load_res(0, 0)

            def turn(q, par, first, more):
                if more:
                    sp.wait_ge(x_split, 2 * q + 2)
                    load_x(q + 1)
                if not first:
                    store(q - 1, 1 - par, q)
                if more:
                    if not first:
                        sp.wait_ge(stored, 16 * q)
                    load_res(q + 1, 1 - par)

            run(sp, turn)
            store(B - 1, 1, B)
            sp.wait_ge(stored, 16 * B)

        @block.tensor
        def _(pe):
            pe.wait_ge(s_loaded, 16 * N_S)
            pe.wait_ge(ident_made, 2)
            pe.wait_ge(pick_made, 4)

            def use(kind, k, n, s, par):
                if kind == "l":
                    pe.wait_ge(x_loaded, 16 * s + 16)
                if kind == "t" and k == 0:
                    pe.wait_ge(w_ready, s + 1)
                if kind == "b" and k == 0:
                    pe.wait_ge(wTr_ready, 2 * s + 2)
                if kind == "y":
                    pe.wait_ge(y_read, s + 1)
                if not (isinstance(n, int) and n == 0):
                    pe.wait_ge(sm_read, n)
                if kind == "l":
                    for t in range(NT):
                        last = nc.tensor.matmul(sm[0:T, 0, t * E:(t + 1) * E], xT[:, t * T:(t + 1) * T], wr[:],
                                                start=True, stop=True)
                elif kind == "t":
                    for t in range(3):
                        last = nc.tensor.transpose(sm[0:E, 0, t * T:(t + 1) * T], w[:, 3 * k + t], ident[0:T, 0:T])
                elif kind == "b":
                    for g in range(2):
                        last = nc.tensor.matmul(sm[:, g, 0:W], pick[:, k], wTr[:, par, cols(g)], start=True, stop=True)
                else:
                    for t in range(NT):
                        last = nc.tensor.transpose(sm[0:T, t // 3, t % 3 * D:(t % 3 + 1) * D],
                                                   yT[:, t * T:(t + 1) * T], ident[:])
                last.then_inc(sm_done, 1)

            for n, (kind, k) in enumerate((("l", 0), ("t", 0), ("t", 1), ("b", 0))):
                use(kind, k, n, 0, 0)

            def turn(q, par, first, more):
                steps = {slot: (kind, k, n) for kind, k, slot, n in turn_uses(q, first, more)}

                def up_layer(u):
                    e, j = u // J, u % J
                    if u == 0:
                        pe.wait_ge(x_split, 2 * q + 2)
                    if first and j == 0:
                        pe.wait_ge(wlo_ready, 2 * e + 2)
                    if not (first and u < 2):
                        pe.wait_ge(raw_ready, UNITS * q + u - 1)
                    for wp, xp in PASSES:
                        for g in range(2):
                            last = nc.tensor.matmul(up[u % 2][:, g, 0:W], w1r[:, wp, e, j * 128:(j + 1) * 128],
                                                    xr[:, par, xp, cols(g)], start=(wp == 0 and xp == 0), stop=(xp == 1))
                    last.then_inc(up_done, 1)

                def down_layer(u):
                    v = u % UNITS
                    e, j = v // J, v % J
                    if v == 0:
                        if not first:
                            pe.wait_ge(y_read, q)
                        for g in range(2):
                            nc.tensor.matmul(y[:, g, 0:W], b2[:], wT[:, par, cols(g)], start=True, stop=False)
                    lo_made(pe, q, u)
                    for wp, hp in PASSES:
                        for g in range(2):
                            last = nc.tensor.matmul(y[:, g, 0:W], w2r[:, wp, e, j * D:(j + 1) * D],
                                                    (hi, lo)[hp][:, v % (LAG + 1), cols(g)], start=False,
                                                    stop=(v == UNITS - 1 and hp == 1))
                    last.then_inc(down_done, 1)

                for u in range(UNITS):
                    up_layer(u)
                    if not (first and u < LAG):
                        down_layer(u - LAG)
                    if u in steps:
                        kind, k, n = steps[u]
                        ahead = kind in "lt" or (kind, k) == ("b", 0)
                        if kind == "y":
                            use(kind, k, n, q - 1, 1 - par)
                        elif ahead:
                            use(kind, k, n, q + 1, 1 - par)
                        else:
                            use(kind, k, n, q, par)
                if not more:
                    for u in range(UNITS - LAG, UNITS):
                        down_layer(u)
                    use("y", 0, n_last, q, par)

            n_last = turn_uses(B - 1, False, False)[-1][3] + 1
            run(pe, turn)

        @block.scalar
        def _(act):
            act.wait_ge(s_loaded, 16 * N_S)

            def split_w(e):
                for src, dst, sem in ((w1, w1r, w1_loaded), (w2, w2r, w2_loaded)):
                    act.wait_ge(sem[e], 16)
                    nc.scalar.activation(dst[:, 0, e], src[:, e], ACT.Copy).then_inc(whi_ready, 1)

            def softmax_gap(s):
                if top == 2:
                    act.wait_ge(gap_ready, s + 1)
                    nc.scalar.activation(gate[:, 1], gate[:, 0], ACT.Exp).then_inc(exp_ready, 1)

            def spread(e, n, q, first):
                act.wait_ge(sm_done, n + 1)
                if not (first and e < 2):
                    act.wait_ge(scaled_ready, UNITS * q + J * (e - 1))
                nc.scalar.activation(split(wide_w[:, e % 2]), two(sm), ACT.Copy).then_inc(sm_read, 1)

            softmax_gap(0)
            split_w(0)
            spread(0, 3, 0, True)

            def turn(q, par, first, more):
                steps = {}
                for kind, k, slot, n in turn_uses(q, first, more):
                    if kind == "b":
                        steps[slot + 1] = lambda k=k, n=n: spread(k, n, q if k else q + 1, first and k > 0)

                def high(u):
                    v = u % UNITS
                    act.wait_ge(scaled_ready, UNITS * q + u + 1)
                    if not (first and u < LAG + 1):
                        act.wait_ge(down_done, UNITS * q + u - LAG)
                    nc.scalar.activation(hi[:, v % (LAG + 1)], scaled[:, v % 2], ACT.Copy).then_inc(hi_ready, 1)

                for u in range(UNITS):
                    act.wait_ge(up_done, UNITS * q + u + 1)
                    if not (first and u < 2):
                        act.wait_ge(scaled_ready, UNITS * q + u - 1)
                    nc.scalar.activation(split(raw[:, u % 2]), two(up[u % 2]), ACT.Gelu,
                                         bias=b1[:, u // J, u % J:u % J + 1]).then_inc(raw_ready, 1)
                    if not (first and u == 0):
                        high(u - 1)
                    if first and u % J == 0 and u // J + 1 < E:
                        split_w(u // J + 1)
                    if u in steps:
                        steps[u]()
                    if more and u == 14:
                        softmax_gap(q + 1)
                if not more:
                    high(UNITS - 1)

            run(act, turn)

        @block.gpsimd
        def _(pool):
            nc.gpsimd.memset(wTr[:].bitcast(F32), 0.0).then_inc(zeroed, 1)
            nc.gpsimd.memset(zero[:], 0.0).then_inc(zeroed, 1)
            make_identity(nc, pool, ident, ident_made)
            nc.gpsimd.iota(iota_i[:], pattern=[[1, E]], base=0, channel_multiplier=0).then_inc(iota_made, 1)
            nc.gpsimd.memset(pick_f[:], 0.0).then_inc(pick_made, 1)
            pool.wait_ge(pick_made, 1)
            for r in range(2):
                nc.gpsimd.affine_select(out=pick_f[:], in_=pick_f[:], compare_op=ALU.not_equal, fill=1.0,
                                        base=-LO * r, pattern=[[-1, E], [0, 128]], channel_multiplier=1).then_inc(pick_made, 1)
                pool.wait_ge(pick_made, r + 2)

            def split_x(s, par, logits):
                pool.wait_ge(x_loaded, 16 * s + 16)
                if not (isinstance(s, int) and s < 2):
                    pool.wait_ge(up_done, UNITS * (s - 1))
                nc.gpsimd.tensor_tensor(xr[:, par, 0], xT[:], zero[:].to_broadcast([D, L]), ALU.add).then_inc(x_split, 1)
                pool.wait_ge(sm_done, logits + 1)
                pool.wait_ge(x_split, 2 * s + 1)
                nc.gpsimd.tensor_tensor(xr[:, par, 1], xT[:], xr[:, par, 0], ALU.subtract).then_inc(x_split, 1)

            pool.wait_ge(zeroed, 2)
            split_x(0, 0, 0)

            def turn(q, par, first, more):
                for u in range(1, UNITS, 2):
                    pool.wait_ge(hi_ready, UNITS * q + u + 1)
                    nc.gpsimd.tensor_tensor(lo[:, u % (LAG + 1)], scaled[:, u % 2], hi[:, u % (LAG + 1)],
                                            ALU.subtract).then_inc(lo_by_pool, 1)
                    if u != 15 or not more:
                        continue
                    split_x(q + 1, 1 - par, [n for kind, k, slot, n in turn_uses(q, first, more) if kind == "l"][0])

            run(pool, turn)

        @block.vector
        def _(dve):
            dve.wait_ge(iota_made, 1)
            nc.vector.tensor_copy(iota[:], iota_i[:]).then_inc(iota_made, 1)
            dve.wait_ge(pick_made, 3)
            nc.vector.tensor_copy(pick[:], pick_f[:]).then_inc(pick_made, 1)
            dve.wait_ge(iota_made, 2)
            dve.wait_ge(s_loaded, 16 * N_S)
            dve.wait_ge(zeroed, 2)
            wide = [T, NT, E]
            SMALL = 3 if top == 1 else 8

            def split_w(e):
                for i, (src, dst) in enumerate(((w1, w1r), (w2, w2r))):
                    dve.wait_ge(whi_ready, 2 * e + i + 1)
                    nc.vector.tensor_tensor(dst[:, 1, e], src[:, e], dst[:, 0, e], ALU.subtract).then_inc(wlo_ready, 1)

            def pick_experts(s, n, step):
                dve.wait_ge(sm_done, n + 1)
                nc.vector.tensor_tensor(lg[:], sm[0:T, 0, 0:NT * E].rearrange("p (k e) -> p k e", e=E),
                                        br[:].unsqueeze(1).to_broadcast(wide), ALU.add).then_inc(lg_ready, 1)
                dve.wait_ge(lg_ready, s + 1)
                dve.sem_inc(sm_read, 1)
                nc.vector.memset(placef[:], 0.0)
                for k in range(NT):
                    ins = nc.vector.max(best[:, k], lg[:, k])
                step(ins)
                nc.vector.memset(placef[:], 0.0)
                for k in range(NT):
                    ins = nc.vector.max_index(place[:, k], best[:, k], lg[:, k])
                step(ins)
                step(nc.vector.tensor_copy(placef[:], place[:]))
                if top == 1:
                    nc.vector.tensor_tensor(w[:], iota[:].unsqueeze(1).to_broadcast(wide),
                                            placef[:, :, 0:1].to_broadcast(wide), ALU.is_equal).then_inc(w_ready, 1)
                else:
                    nc.vector.tensor_tensor(gate[:, 0], best[:, :, 1], best[:, :, 0], ALU.subtract).then_inc(gap_ready, 1)
                    for r in range(2):
                        last = nc.vector.tensor_tensor(mask[:, r], iota[:].unsqueeze(1).to_broadcast(wide),
                                                       placef[:, :, r:r + 1].to_broadcast(wide), ALU.is_equal)
                    step(last)

            def weigh(s, step):
                if top == 1:
                    return
                dve.wait_ge(exp_ready, s + 1)
                step(nc.vector.tensor_scalar(gate[:, 0], gate[:, 1], 1.0, None, ALU.add))
                step(nc.vector.reciprocal(gate[:, 0], gate[:, 0]))
                step(nc.vector.tensor_tensor(gate[:, 1], gate[:, 1], gate[:, 0], ALU.mult))
                for r in range(2):
                    last = nc.vector.tensor_tensor(mask[:, r], mask[:, r],
                                                   gate[:, r].unsqueeze(2).to_broadcast(wide), ALU.mult)
                step(last)
                nc.vector.tensor_tensor(w[:], mask[:, 0], mask[:, 1], ALU.add).then_inc(w_ready, 1)

            def gates_turned(par, r, n):
                dve.wait_ge(sm_done, n + 1)
                nc.vector.tensor_copy(wT[:, par, r * H:(r + 1) * H], sm[0:E, 0, 0:H]).then_inc(sm_read, 1)

            def split_gates(s, par, n):
                dve.wait_ge(sm_read, n + 1)
                nc.vector.tensor_copy(wTr[0:E, par], wT[:, par]).then_inc(wTr_ready, 1)
                dve.wait_ge(wTr_ready, 2 * s + 1)
                nc.vector.tensor_tensor(wTr[LO:LO + E, par], wT[:, par], wTr[0:E, par], ALU.subtract).then_inc(wTr_ready, 1)

            def read_y(s):
                dve.wait_ge(down_done, UNITS * (s + 1))
                nc.vector.tensor_copy(split(yT[:]), two(y)).then_inc(y_read, 1)

            def add_res(par, n, loads):
                dve.wait_ge(sm_done, n + 1)
                dve.wait_ge(res_loaded[par], loads)
                half = res[:, par].rearrange("p (r k) c -> p r (k c)", r=2)
                nc.vector.tensor_tensor(half, half, sm[0:T, :, 0:3 * D], ALU.add).then_inc(res_done, 1)

            step = chain(dve, dve_step, 0)
            pick_experts(0, 0, step)
            weigh(0, step)
            for r in range(2):
                gates_turned(0, r, 1 + r)
            split_gates(0, 0, 2)
            split_w(0)
            assert step.count[0] == SMALL, step.count[0]

            def turn(q, par, first, more):
                f = q + 1
                step = chain(dve, dve_step, SMALL * f)
                at = {(kind, k): (slot + 1, n) for kind, k, slot, n in turn_uses(q, first, more)}
                steps = {}
                if more:
                    steps[at["l", 0][0]] = lambda: pick_experts(f, at["l", 0][1], step)
                    steps[15] = lambda: weigh(f, step)
                    for r in range(2):
                        steps[at["t", r][0]] = lambda r=r: gates_turned(1 - par, r, at["t", r][1])
                    steps[26] = lambda: split_gates(f, 1 - par, at["t", 1][1])
                if not first:
                    def finish():
                        add_res(1 - par, at["y", 0][1], 8 * q + 8 * par)
                        dve.wait_ge(res_done, q)
                        dve.sem_inc(sm_read, 1)
                    steps[LAG - 1] = lambda: read_y(q - 1)
                    steps[at["y", 0][0]] = finish
                spread_at = {k: n for kind, k, slot, n in turn_uses(q, first, more) if kind == "b" and k}

                def low(u):
                    v = u % UNITS
                    dve.wait_ge(hi_ready, UNITS * q + u + 1)
                    nc.vector.tensor_tensor(lo[:, v % (LAG + 1)], scaled[:, v % 2], hi[:, v % (LAG + 1)],
                                            ALU.subtract).then_inc(lo_ready, 1)

                for u in range(UNITS):
                    e = u // J
                    if u % J == 0:
                        dve.wait_ge(sm_read, (spread_at[e] if e else (3 if first else PRO - 2 + PER * q)) + 1)
                    dve.wait_ge(raw_ready, UNITS * q + u + 1)
                    if not (first and u < 2):
                        lo_made(dve, q, u - 2)
                    nc.vector.tensor_tensor(scaled[:, u % 2], raw[:, u % 2], wide_w[:, e % 2], ALU.mult).then_inc(scaled_ready, 1)
                    if u % 2:
                        low(u - 1)
                    if first and u % J == 0 and e + 1 < E:
                        split_w(e + 1)
                    if u in steps:
                        steps[u]()
                if not more:
                    read_y(q)
                    add_res(par, turn_uses(q, first, more)[-1][3] + 1, 16 * (B // 2))

            run(dve, turn)


def stage_attn(nc, a, xT_s, h_in, h_out):
    UNITS, LAG = HEADS * NT, 3
    GROUPS = UNITS // 3
    W = H + 1
    SCALE = DH ** -0.5
    with ExitStack() as ctx:
        m = Mem(nc, ctx, "at")
        w_qkv = m.sb("w_qkv", [D, 3, HEADS * DH])
        w_g, b_g = m.sb("w_g", [D, HEADS]), m.sb("b_g", [T, HEADS])
        w_o = m.sb("w_o", [2 * DH, HEADS, D])
        b_o = m.sb("b_o", [T, D])
        cos, sin = m.sb("cos", [T, NT, DH // 4]), m.sb("sin", [T, NT, DH // 4])
        ident = m.sb("ident", [128, 128])
        xT = m.sb("xT", [D, L])
        raw = m.sb("raw", [T, 2, HEADS, DH])
        tmp = m.sb("tmp", [T, HEADS, DH // 2])
        roped = m.sb("roped", [T, 2, NT, 2, HEADS, DH])
        v = m.sb("v", [T, 2, NT, HEADS, 2 * DH], F32R)
        q2 = m.sb("q2", [2 * DH, 2, L + 2], F32R)
        khh, kll = m.sb("khh", [2 * DH, 2, L + 2], F32R), m.sb("kll", [2 * DH, 2, L + 2], F32R)
        pr = m.sb("pr", [T, 3, L])
        phi, plo = m.sb("phi", [T, 2, NT, W], F32R), m.sb("plo", [T, 2, NT, W], F32R)
        oT = m.sb("oT", [2 * DH, HEADS, L])
        mx, nm, rs, ri, gs = (m.sb(n, [T, 4]) for n in ("mx", "nm", "rs", "ri", "gs"))
        gt, ge = m.sb("gt", [T, NT, HEADS]), m.sb("ge", [T, NT, HEADS])
        gate = m.sb("gate", [T, 2, NT, HEADS])
        res, ob = m.sb("res", [T, NT, D]), m.sb("ob", [T, NT, D])
        sc = [m.ps(f"sc{s}") for s in range(2)]
        pt = m.ps("pt")
        po = m.ps("po", (128, 512))
        pp = m.ps("pp", (128, 512))

        w_loaded, ident_made, pads = m.sem("w_loaded"), m.sem("ident_made"), m.sem("pads")
        x_loaded, res_loaded = m.sem("x_loaded"), m.sem("res_loaded")
        scored, maxed, negated, exped = m.sem("scored"), m.sem("maxed"), m.sem("negated"), m.sem("exped")
        inverted, scaled, gs_ready, turned = m.sem("inverted"), m.sem("scaled"), m.sem("gs_ready"), m.sem("turned")
        hi_ready, lo_ready = m.sem("hi_ready"), m.sem("lo_ready")
        po_done, po_free, pv_done, out_evac = m.sem("po_done"), m.sem("po_free"), m.sem("pv_done"), m.sem("out_evac")
        pp_done, pp_free, pp_act = m.sem("pp_done"), m.sem("pp_free"), m.sem("pp_act")
        roped_ready, rope_step = m.sem("roped_ready"), m.sem("rope_step")
        gt_ready, ge_ready, gate_step, gate_ready = m.sem("gt_ready"), m.sem("ge_ready"), m.sem("gate_step"), m.sem("gate_ready")
        res_step, stored = m.sem("res_step"), m.sem("stored")
        N_W = 7

        PRO, PER = 23, 51
        GATES = 46

        def pp_at(q, hd, j, more):
            if not more:
                return PRO + PER * q + 4 * hd + j
            return PRO + PER * q + (7 * hd + j if hd < 7 else 47 + j)

        def act_at(q, hd, j, more):
            if not more:
                return PRO - 1 + (PER - 1) * q + 4 * hd + j
            return PRO - 1 + (PER - 1) * q + (7 * hd + j if hd < 7 else 46 + j)

        PO = 22

        def po_at(q, at):
            return 14 + PO * (q - 1) + at

        def turns(turn):
            def run(eng):
                turn(0, 0, True, True)
                with eng.Fori(0, (B - 2) // 2) as i:
                    turn(2 * i + 1, 1, False, True)
                    turn(2 * i + 2, 0, False, True)
                turn(B - 1, 1, False, False)
            return run

        HEAD_AT, PROJECT_AT = (0, 2, 4, 6), (7, 8, 10)

        def plan(q, par, more, turn_head, project, gates):
            steps = {}
            for hd in range(HEADS):
                nh, npar = (hd + 1, par) if hd < HEADS - 1 else (0, 1 - par)
                if hd < HEADS - 1 or more:
                    for j, off in enumerate(HEAD_AT):
                        steps[12 * hd + off] = lambda hd=hd, nh=nh, npar=npar, j=j: turn_head(
                            pp_at(q, hd, j, more), act_at(q, hd, j, more), q, hd, nh, npar, j // 2, j % 2)
                if more and hd < NT:
                    for part, off in enumerate(PROJECT_AT):
                        steps[12 * hd + off] = lambda k=hd, part=part: project(
                            pp_at(q, k, 4 + part, more), act_at(q, k, 4 + part, more), q + 1, 1 - par, k, part)
            if more:
                steps[12 * NT + PROJECT_AT[0]] = lambda: gates(PRO + PER * q + GATES, q + 1, 1 - par)
            return steps

        def nothing():
            pass

        def prologue(turn_head, project, gates):
            for k in range(NT):
                for part in range(3):
                    project(3 * k + part, 3 * k + part, 0, 0, k, part)
            gates(18, 0, 0)
            for j in range(4):
                turn_head(19 + j, 18 + j, -1, HEADS - 1, 0, 0, j // 2, j % 2)

        def po_uses(q, u, first, after=False):
            early = {0: ("v", -2), 1: ("o", 0), 2: ("o", 1), 3: ("v", -1), 4: ("o", 2), 5: ("o", 3), 7: ("o", 4), 8: ("o", 5)}
            if u in early:
                return [] if first else [(*early[u], po_at(q, list(early).index(u) + (1 if u > 6 and not after else 0)))]
            if u % 3 or u < 6 or after:
                return []
            gi = (u - 6) // 3
            return [("v", gi, gi if first else po_at(q, 8 + gi - (2 if gi == 0 else 0)))]

        def rows_of_head(nh):
            own, other = nh % 2 * DH, (1 - nh % 2) * DH
            return slice(own, own + DH), slice(other, other + DH)

        block = m.block()

        @block.sync
        def _(sp):
            for dst, src in ((w_qkv[:], a["w_qkv"]), (w_g[:], a["w_gates"]), (b_g[:], rows(a["b_gates"], T)),
                             (w_o[:], a["w_out2"]), (b_o[:], rows(a["b_out"], T)),
                             (cos[:], a["rope_cos"]), (sin[:], a["rope_sin"])):
                sp.dma_start(dst, src).then_inc(w_loaded, 16)
            sp.dma_start(xT[:], xT_s[0]).then_inc(x_loaded, 16)
            def rows_of(h, b):
                return h[b].rearrange("(k p) c -> p k c", p=T)

            def next_x(b):
                sp.wait_ge(gt_ready, b)
                sp.dma_start(xT[:], xT_s[b]).then_inc(x_loaded, 16)

            def store(b):
                sp.wait_ge(res_step, 2 * b + 2)
                sp.dma_start(rows_of(h_out, b), res[:]).then_inc(stored, 16)

            sp.dma_start(res[:], rows_of(h_in, 0)).then_inc(res_loaded, 16)
            next_x(1)
            with sp.Fori(0, B - 2) as i:
                next_x(i + 2)
                store(i)
                sp.wait_ge(stored, 16 * i + 16)
                sp.dma_start(res[:], rows_of(h_in, i + 1)).then_inc(res_loaded, 16)
            store(B - 2)
            sp.wait_ge(stored, 16 * (B - 1))
            sp.dma_start(res[:], rows_of(h_in, B - 1)).then_inc(res_loaded, 16)
            store(B - 1)
            sp.wait_ge(stored, 16 * B)

        @block.tensor
        def _(pe):
            pe.wait_ge(w_loaded, 16 * N_W)
            pe.wait_ge(ident_made, 2)
            pe.wait_ge(pads, 2)

            def turn_head(n, na, q, hd, nh, par, g, qk):
                if g == 0 and qk == 0 and nh == 0:
                    pe.wait_ge(roped_ready, 2 * NT * (q + 2))
                pe.wait_ge(pp_free, n)
                for k in range(3):
                    pair = roped[:, par, 3 * g + k, qk, nh // 2 * 2:nh // 2 * 2 + 2].rearrange("p h c -> p (h c)")
                    last = nc.tensor.transpose(pp[:, k * T:(k + 1) * T], pair, ident[0:T, 0:T])
                last.then_inc(pp_done, 1)

            def project(n, na, b, par, k, part):
                if k == 0 and part == 0:
                    pe.wait_ge(x_loaded, 16 * b + 16)
                pe.wait_ge(pp_free, n)
                nc.tensor.matmul(pp[0:T, :], xT[:, k * T:(k + 1) * T], w_qkv[:, part], start=True,
                                 stop=True).then_inc(pp_done, 1)

            def gates(n, b, par):
                pe.wait_ge(pp_free, n)
                for k in range(NT):
                    last = nc.tensor.matmul(pp[0:T, k * HEADS:(k + 1) * HEADS], xT[:, k * T:(k + 1) * T], w_g[:],
                                            start=True, stop=True)
                last.then_inc(pp_done, 1)

            prologue(turn_head, project, gates)

            def turn(q, par, first, more):
                steps = plan(q, par, more, turn_head, project, gates)

                def scores(u):
                    hd, k = u // NT, u % NT
                    if k == 0:
                        pe.wait_ge(pp_free, (pp_at(q, hd - 1, 3, more) if hd else PRO + PER * q - 1) + 1)
                    if not first or u >= 2:
                        pe.wait_ge(exped, UNITS * q + u - 1)
                    for g in range(2):
                        for p, kk in enumerate((khh, kll)):
                            last = nc.tensor.matmul(sc[u % 2][0:T, g, 0:W], q2[:, hd % 2, k * T:(k + 1) * T],
                                                    kk[:, hd % 2, g * (L - W):g * (L - W) + W],
                                                    start=(p == 0), stop=(p == 1))
                    last.then_inc(scored, 1)

                def turn_probs(u):
                    pe.wait_ge(scaled, UNITS * q + u + 1)
                    for g in range(2):
                        if not (first and u == 0):
                            pe.wait_ge(lo_ready, 2 * (UNITS * q + u) - 1 + g)
                        for jk in range(3):
                            last = nc.tensor.transpose(pt[0:T, g, jk * T:(jk + 1) * T],
                                                       pr[:, u % 3, (3 * g + jk) * T:(3 * g + jk + 1) * T], ident[0:T, 0:T])
                        last.then_inc(turned, 1)

                def times_v(gi, at):
                    hd, vp = gi // 2 % HEADS, par if gi >= 0 else 1 - par
                    pe.wait_ge(lo_ready, 2 * (UNITS * q + 3 * gi + 3))
                    pe.wait_ge(po_free, at)
                    for jk in range(NT):
                        for p, part in enumerate((phi, plo)):
                            last = nc.tensor.matmul(po[:, 0:W], v[:, vp, jk, hd], part[:, gi % 2, jk],
                                                    start=(jk == 0 and p == 0), stop=(jk == NT - 1 and p == 1))
                    last.then_inc(po_done, 1)

                def out_tile(k, at):
                    pe.wait_ge(po_free, at)
                    for hd in range(HEADS):
                        last = nc.tensor.matmul(po[0:T, 0:D], oT[:, hd, k * T:(k + 1) * T], w_o[:, hd],
                                                start=(hd == 0), stop=(hd == HEADS - 1))
                    last.then_inc(po_done, 1)

                pe_slots(q, first, more, scores, turn_probs, times_v, out_tile, steps)

            def pe_slots(q, first, more, scores, turn_probs, times_v, out_tile, steps):
                for u in range(UNITS):
                    scores(u)
                    steps.get(2 * u, nothing)()
                    if not first or u >= LAG:
                        turn_probs(u - LAG)
                    for kind, x, at in po_uses(q, u, first):
                        (times_v if kind == "v" else out_tile)(x, at)
                    steps.get(2 * u + 1, nothing)()
                if not more:
                    for u in range(UNITS, UNITS + 9):
                        if u < UNITS + LAG:
                            turn_probs(u - LAG)
                        for kind, x, at in po_uses(q + 1, u - UNITS, False, True):
                            (times_v if kind == "v" else out_tile)((x + GROUPS) if kind == "v" else x, at)

            turns(turn)(pe)

        @block.scalar
        def _(act):
            act.wait_ge(w_loaded, 16 * N_W)
            act.wait_ge(pads, 2)

            def turn_head(n, na, q, hd, nh, par, g, qk):
                act.wait_ge(pp_done, n + 1)
                if not (isinstance(q, int) and q < 0):
                    act.wait_ge(scored, UNITS * q + NT * hd)
                own, other = rows_of_head(nh)
                at = slice(g * H, (g + 1) * H)
                if qk == 0:
                    nc.scalar.activation(q2[own, nh % 2, at], pp[own, 0:H], ACT.Copy).then_inc(pp_act, 1)
                else:
                    nc.scalar.activation(khh[own, nh % 2, at], pp[own, 0:H], ACT.Copy)
                    nc.scalar.activation(khh[other, nh % 2, at], pp[own, 0:H], ACT.Copy).then_inc(pp_act, 1)

            def project(n, na, b, par, k, part):
                act.wait_ge(pp_done, n + 1)
                if part < 2:
                    if not (isinstance(b, int) and b == 0 and k == 0):
                        act.wait_ge(roped_ready, 2 * (NT * b + k) - 1 + part)
                    nc.scalar.activation(raw[:, part].rearrange("p h c -> p (h c)"), pp[0:T, :], ACT.Copy).then_inc(pp_act, 1)
                    act.wait_ge(pp_act, na + 1)
                    act.sem_inc(pp_free, 1)
                else:
                    if not (isinstance(b, int) and b < 2):
                        act.wait_ge(pv_done, GROUPS * (b - 1))
                    nc.scalar.activation(v[:, par, k, :, 0:DH], pp[0:T, :].rearrange("p (h c) -> p h c", h=HEADS),
                                         ACT.Copy).then_inc(pp_act, 1)

            def gates(n, b, par):
                act.wait_ge(gt_ready, b + 1)
                nc.scalar.activation(ge[:], gt[:], ACT.Exp, scale=-1.0).then_inc(ge_ready, 1)

            prologue(turn_head, project, gates)

            def turn(q, par, first, more):
                steps = plan(q, par, more, turn_head, project, gates)

                def hi(u):
                    U = UNITS * q + u
                    for g in range(2):
                        act.wait_ge(turned, 2 * U + g + 1)
                        if u % 3 == 0 and g == 0 and not (first and u < 6):
                            act.wait_ge(pv_done, GROUPS * q + u // 3 - 1)
                        nc.scalar.activation(phi[:, u // 3 % 2, 3 * g:3 * g + 3, u % 3 * T:(u % 3 + 1) * T],
                                             pt[0:T, g, 0:3 * T].rearrange("p (k t) -> p k t", k=3),
                                             ACT.Copy).then_inc(hi_ready, 1)

                def exp(u):
                    U = UNITS * q + u
                    act.wait_ge(negated, U + 1)
                    if not (first and u < 3):
                        act.wait_ge(turned, 2 * U - 4)
                    src = bass.AP(sc[u % 2], 0, [[1024, T], [513, 2], [1, H]])
                    nc.scalar.activation(split(pr[:, u % 3]), src, ACT.Exp, bias=nm[:, u % 4:u % 4 + 1], scale=SCALE,
                                         accum_out=rs[:, u % 4:u % 4 + 1]).then_inc(exped, 1)

                def evac(kind, x, at):
                    act.wait_ge(po_done, at + 1)
                    if kind == "v":
                        hd, g = x // 2 % HEADS, x % 2
                        nc.scalar.activation(oT[:, hd, g * H:(g + 1) * H], po[:, 0:H], ACT.Copy).then_inc(pv_done, 1)
                        act.wait_ge(pv_done, GROUPS * q + x + 1)
                    else:
                        if x == 0 and not (isinstance(q, int) and q == 1):
                            act.wait_ge(stored, 16 * (q - 1))
                        nc.scalar.activation(ob[:, x], po[0:T, 0:D], ACT.Copy).then_inc(out_evac, 1)
                        act.wait_ge(out_evac, NT * (q - 1) + x + 1)
                    act.sem_inc(po_free, 1)

                for u in range(UNITS):
                    steps.get(2 * u, nothing)()
                    if not first or u >= LAG:
                        hi(u - LAG)
                    exp(u)
                    for x in po_uses(q, u, first):
                        evac(*x)
                    steps.get(2 * u + 1, nothing)()
                if not more:
                    for u in range(UNITS, UNITS + 9):
                        if u < UNITS + LAG:
                            hi(u - LAG)
                        for kind, x, at in po_uses(q + 1, u - UNITS, False, True):
                            if kind == "v":
                                evac(kind, x + GROUPS, at)
                            else:
                                if x == 0:
                                    act.wait_ge(stored, 16 * q)
                                act.wait_ge(po_done, at + 1)
                                nc.scalar.activation(ob[:, x], po[0:T, 0:D], ACT.Copy).then_inc(out_evac, 1)
                                act.wait_ge(out_evac, NT * q + x + 1)
                                act.sem_inc(po_free, 1)

            turns(turn)(act)

        @block.vector
        def _(dve):
            for part in (phi, plo):
                nc.vector.memset(part[:, :, :, H:W].bitcast(F32), 0.0).then_inc(pads, 1)
            dve.wait_ge(w_loaded, 16 * N_W)

            def turn_head(n, na, q, hd, nh, par, g, qk):
                dve.wait_ge(pp_act, na + 1)
                own, other = rows_of_head(nh)
                at = slice(g * H, (g + 1) * H)
                if qk == 0:
                    nc.vector.tensor_tensor(q2[other, nh % 2, at], pp[own, 0:H], q2[own, nh % 2, at],
                                            ALU.subtract).then_inc(pp_free, 1)
                else:
                    nc.vector.tensor_tensor(kll[other, nh % 2, at], pp[own, 0:H], khh[own, nh % 2, at], ALU.subtract)
                    nc.vector.tensor_tensor(kll[own, nh % 2, at], pp[own, 0:H], khh[own, nh % 2, at],
                                            ALU.subtract).then_inc(pp_free, 1)

            def project(n, na, b, par, k, part):
                if part == 2:
                    dve.wait_ge(pp_act, na + 1)
                    nc.vector.tensor_tensor(v[:, par, k, :, DH:2 * DH], pp[0:T, :].rearrange("p (h c) -> p h c", h=HEADS),
                                            v[:, par, k, :, 0:DH], ALU.subtract).then_inc(pp_free, 1)

            def gates(n, b, par):
                dve.wait_ge(pp_done, n + 1)
                nc.vector.tensor_tensor(gt[:], pp[0:T, 0:NT * HEADS].rearrange("p (k h) -> p k h", k=NT),
                                        b_g[:].unsqueeze(1).to_broadcast([T, NT, HEADS]), ALU.add).then_inc(gt_ready, 1)
                dve.wait_ge(gt_ready, b + 1)
                dve.sem_inc(pp_free, 1)
                dve.wait_ge(ge_ready, b + 1)
                nc.vector.tensor_scalar(ge[:], ge[:], 1.0, None, ALU.add).then_inc(gate_step, 1)
                dve.wait_ge(gate_step, b + 1)
                nc.vector.reciprocal(gate[:, par], ge[:]).then_inc(gate_ready, 1)

            prologue(turn_head, project, gates)

            def turn(q, par, first, more):
                steps = plan(q, par, more, turn_head, project, gates)

                def invert(u):
                    U = UNITS * q + u
                    dve.wait_ge(exped, U + 1)
                    if not (first and u < 4):
                        dve.wait_ge(gs_ready, U - 3)
                    c = u % 4
                    nc.vector.reciprocal(ri[:, c:c + 1], rs[:, c:c + 1]).then_inc(inverted, 1)

                def lo(u):
                    U = UNITS * q + u
                    for g in range(2):
                        dve.wait_ge(hi_ready, 2 * U + g + 1)
                        dst = (slice(None), u // 3 % 2, slice(3 * g, 3 * g + 3), slice(u % 3 * T, (u % 3 + 1) * T))
                        nc.vector.tensor_tensor(plo[dst], pt[0:T, g, 0:3 * T].rearrange("p (k t) -> p k t", k=3),
                                                phi[dst], ALU.subtract).then_inc(lo_ready, 1)

                for u in range(UNITS):
                    U = UNITS * q + u
                    c = u % 4
                    dve.wait_ge(scored, U + 1)
                    src = bass.AP(sc[u % 2], 0, [[1024, T], [513, 2], [1, H]])
                    nc.vector.tensor_reduce(mx[:, c:c + 1], src, mybir.AxisListType.XY, ALU.max).then_inc(maxed, 1)
                    if not first or u >= 1:
                        invert(u - 1)
                    dve.wait_ge(maxed, U + 1)
                    nc.vector.tensor_scalar(nm[:, c:c + 1], mx[:, c:c + 1], -SCALE, None, ALU.mult).then_inc(negated, 1)
                    steps.get(2 * u, nothing)()
                    if not first or u >= LAG:
                        lo(u - LAG)
                    steps.get(2 * u + 1, nothing)()
                if not more:
                    invert(UNITS - 1)
                    for u in range(UNITS, UNITS + LAG):
                        lo(u - LAG)

            turns(turn)(dve)

        @block.gpsimd
        def _(pool):
            make_identity(nc, pool, ident, ident_made)
            pool.wait_ge(w_loaded, 16 * N_W)
            OPS = 4

            def rope(b, par, k, part, third):
                n = NT * b + k
                def quarters(ap):
                    return ap.rearrange("p h (r c) -> p h r c", r=2)

                wide = [T, HEADS, 2, DH // 4]
                c = cos[:, k].unsqueeze(1).unsqueeze(1).to_broadcast(wide)
                s = sin[:, k].unsqueeze(1).unsqueeze(1).to_broadcast(wide)
                x1, x2 = quarters(raw[:, part, :, 0:DH // 2]), quarters(raw[:, part, :, DH // 2:])
                out = roped[:, par, k, part]
                base = 2 * OPS * n + OPS * part + 2 * third
                if third == 0:
                    pool.wait_ge(pp_act, raw_count(b, k, part))
                m0, m1, op, dst = ((c, s, ALU.subtract, out[:, :, 0:DH // 2]), (s, c, ALU.add, out[:, :, DH // 2:]))[third]
                if third:
                    pool.wait_ge(rope_step, base)
                nc.gpsimd.tensor_tensor(quarters(dst), x1, m0, ALU.mult)
                nc.gpsimd.tensor_tensor(quarters(tmp[:]), x2, m1, ALU.mult).then_inc(rope_step, 1)
                pool.wait_ge(rope_step, base + 1)
                ins = nc.gpsimd.tensor_tensor(dst, dst, tmp[:], op)
                ins.then_inc(rope_step, 1)
                pool.wait_ge(rope_step, base + 2)
                if third:
                    pool.sem_inc(roped_ready, 1)

            def raw_count(b, k, part):
                if isinstance(b, int) and b == 0:
                    return 3 * k + part + 1
                return act_at(b - 1, k, 4 + part, True) + 1

            for k in range(NT):
                for part in range(2):
                    for third in range(2):
                        rope(0, 0, k, part, third)

            def finish(b):
                wide = [T, NT, D]
                pool.wait_ge(res_loaded, 16 * b + 16)
                nc.gpsimd.tensor_tensor(res[:], res[:], b_o[:].unsqueeze(1).to_broadcast(wide), ALU.add).then_inc(res_step, 1)
                pool.wait_ge(res_step, 2 * b + 1)
                pool.wait_ge(out_evac, NT * b + NT)
                nc.gpsimd.tensor_tensor(res[:], res[:], ob[:], ALU.add).then_inc(res_step, 1)
                pool.wait_ge(res_step, 2 * b + 2)

            def turn(q, par, first, more):
                if first:
                    pool.wait_ge(gate_ready, 1)

                def scale(u):
                    U = UNITS * q + u
                    hd, k, c = u // NT % HEADS, u % NT, u % 4
                    pool.wait_ge(inverted, U + 1)
                    gp = par if u >= 0 else 1 - par
                    nc.gpsimd.tensor_tensor(gs[:, c:c + 1], ri[:, c:c + 1], gate[:, gp, k, hd:hd + 1], ALU.mult).then_inc(gs_ready, 1)
                    pool.wait_ge(gs_ready, U + 1)
                    nc.gpsimd.tensor_tensor(pr[:, u % 3], pr[:, u % 3], gs[:, c:c + 1].to_broadcast([T, L]), ALU.mult).then_inc(scaled, 1)

                for u in range(UNITS):
                    if not first or u >= 1:
                        scale(u - 1)
                    if u == 0 and not first:
                        pool.wait_ge(gate_ready, q + 1)
                    if u == 10 and not first:
                        finish(q - 1)
                    if more:
                        k, off = (u - 5) // 6, (u - 5) % 6
                        if 0 <= k < NT and off < 4:
                            rope(q + 1, 1 - par, k, off // 2, off % 2)
                if not more:
                    scale(UNITS - 1)
                    finish(q)

            turns(turn)(pool)



FF = ("Wr", "br", "W1", "b1", "W2", "b2")


def layout(inp):
    import numpy as np
    out = {"x": inp["x"]}
    tok = "L0_tok_"
    for n in ("b_proj", "W_dw", "b_dw", "b_pw", "gamma", "beta"):
        out["tok_" + n] = inp[tok + n]
    out["tok_W_projT"] = inp[tok + "W_proj"].T
    out["tok_W_pwT"] = inp[tok + "W_pw"].T
    for w in ("fw_", "bw_"):
        def g(n):
            return inp["L0_attn_" + w + n]
        proj = g("W_xproj")
        out[w + "W_inT"] = g("W_in").T
        out[w + "W_xprojT"] = np.concatenate([proj[DT_RANK:], proj[DT_RANK:], proj[:DT_RANK]]).T
        out[w + "W_dtT"] = g("W_dt").T
        out[w + "W_outT"] = g("W_out").T
        out[w + "conv_wT"], out[w + "A_log"] = g("conv_w").T, g("A_log")
        out[w + "vec"] = np.stack([g(n).reshape(2, 128).T for n in ("conv_b", "b_dt", "D_skip")], 1)
    out["attn_ln_g"], out["attn_ln_b"] = inp["L0_attn_ln_g"], inp["L0_attn_ln_b"]
    w = inp["L1_attn_w_qkv"].reshape(D, 3, HEADS, DH // 2, 2)
    out["w_qkv"] = np.concatenate([w[:, :2].transpose(0, 1, 2, 4, 3).reshape(D, 2, HEADS * DH),
                                   w[:, 2:].reshape(D, 1, HEADS * DH)], 1)
    w = inp["L1_attn_w_out"].reshape(HEADS, DH, D).transpose(1, 0, 2)
    out["w_out2"] = np.concatenate([w, w], 0)
    for n in ("w_gates", "b_gates", "b_out"):
        out[n] = inp["L1_attn_" + n]
    for st, pre, names in (("f0", "L0_ffn_", FF), ("f1", "L1_ffn_", ("w_r", "b_r") + FF[2:])):
        wr, br, w1, b1, w2, b2 = (inp[pre + n] for n in names)
        out[st + "_Wr"], out[st + "_br"], out[st + "_b2"] = (wr if st == "f0" else wr.T), br, b2
        out[st + "_W1"] = w1.transpose(1, 0, 2)
        out[st + "_b1"] = b1.reshape(E, 4, 128).transpose(2, 0, 1)
        out[st + "_W2"] = w2.reshape(E, 4, 128, D).transpose(2, 0, 1, 3).reshape(128, E, 4 * D)
    out["f1_ln_g"], out["f1_ln_b"] = inp["L1_ffn_ln_g"], inp["L1_ffn_ln_b"]
    half = DH // 2
    inv = np.float32(1.0) / np.float32(10.0) ** (np.arange(0, half, 2, dtype=np.float32) / np.float32(half))
    ang = (np.arange(L, dtype=np.float32)[:, None] * inv[None, :].astype(np.float32)).astype(np.float64)
    for n, fn in (("rope_cos", np.cos), ("rope_sin", np.sin)):
        out[n] = fn(ang).astype(np.float32).reshape(NT, T, half // 2).transpose(1, 0, 2)
    return {k: np.ascontiguousarray(v) for k, v in out.items()}


def build(nc, a, out):
    def scratch(name, *shape):
        return nc.dram_tensor(name, shape, F32, kind="Internal").ap()

    xln, mix, brow = scratch("xln", 2 * B, D, L), scratch("mix", 2 * B, D, L), scratch("brow", 2, D_STATE, L)
    xT = [scratch(f"xT{i}", B, D, L) for i in range(3)]
    h = [scratch(f"h{i}", B, L, D) for i in range(6)]
    stage_tok(nc, a, xln, h[0])
    stage_mamba(nc, a, xln, brow, mix)
    stage_norm(nc, a, "n0", h[0], xT[0], h[1], mixed=mix)
    stage_ffn(nc, a, "f0", 1, xT[0], h[1], h[2])
    stage_norm(nc, a, "n1", h[2], xT[1], h[3])
    stage_attn(nc, a, xT[1], h[3], h[4])
    stage_norm(nc, a, "n2", h[4], xT[2], h[5], affine=(a["f1_ln_g"], a["f1_ln_b"]))
    stage_ffn(nc, a, "f1", 2, xT[2], h[5], out)


def kernel(**inputs):
    import numpy as np
    import concourse.bacc as bacc
    from concourse.bass_utils import run_bass_kernel_spmd

    nc = bacc.Bacc("TRN2", target_bir_lowering=False, num_devices=1)
    arrays, a = {}, {}
    for name, value in layout({k: np.asarray(v) for k, v in inputs.items()}).items():
        arrays[f"in_{name}"] = value
        a[name] = nc.dram_tensor(f"in_{name}", value.shape, mybir.dt.from_np(value.dtype), kind="ExternalInput").ap()
    out = nc.dram_tensor("out_0_dram", (B, L, D), F32, kind="ExternalOutput").ap()
    build(nc, a, out)
    r = run_bass_kernel_spmd(nc, [arrays], core_ids=[0])
    return r.results[0]["out_0_dram"]
```
